# Optimizing a Trainium2 kernel written in Bass

```python
import numpy as np
import jax
import jax.numpy as jnp

def _softmax(x, axis=-1):
    return jax.nn.softmax(x, axis=axis)

def _gelu(x):
    return jax.nn.gelu(x, approximate=True)

def _silu(x):
    return jax.nn.silu(x)

def _sigmoid(x):
    return jax.nn.sigmoid(x)

def _layernorm(x, axis=-1, eps=1e-05):
    m = jnp.mean(x, axis=axis, keepdims=True)
    v = jnp.var(x, axis=axis, keepdims=True)
    return (x - m) / jnp.sqrt(v + eps)

def _scatter_add(tgt, idx, src, axis=0):
    return tgt.at[idx].add(src)

def _segment_sum(src, seg, n):
    return jax.ops.segment_sum(src, seg, n)
kernel_name = 'mk_adaln_d1_jaxref_r4_dfeff8'

def setup_inputs(seed: int=0):
    np.random.seed(seed)
    _w = jnp.asarray

    def _L0_attn_setup():
        import jax, jax.numpy as jnp
        import numpy as np
        B, S, D = (4, 512, 256)

        def givens_rotate(r, x):
            g = r.reshape(-1, 2)
            g = g / jnp.linalg.norm(g, axis=-1, keepdims=True)
            xp = x.reshape(x.shape[:-1] + (x.shape[-1] // 2, 2))
            c, s = (g[:, 0], g[:, 1])
            y0 = c * xp[..., 0] - s * xp[..., 1]
            y1 = c * xp[..., 1] + s * xp[..., 0]
            return jnp.stack([y0, y1], axis=-1).reshape(x.shape)
        key = jax.random.key(seed)
        k1, k2 = jax.random.split(key, 2)
        Q = jax.random.normal(k1, (B, S, D), dtype=jnp.float32)
        rot_w = jax.random.uniform(k2, (3, D), dtype=jnp.float32, minval=-1.0, maxval=1.0)
        scale = jnp.array([np.sqrt(D)], dtype=jnp.float32)
        bias = jnp.zeros((), dtype=jnp.float32)
        return {'Q': Q, 'rot_w': rot_w, 'scale': scale, 'bias': bias}
    _L0_attn_in = _L0_attn_setup()

    def _L0_ffn_setup():
        import jax, jax.numpy as jnp
        import numpy as np
        B, S, D = (4, 1024, 256)
        E, F_EXP = (16, 512)
        F_C = 2.0
        F_SH = 512
        key = jax.random.key(seed)
        ks = jax.random.split(key, 8)
        s = 0.02
        return {'hidden_states': jax.random.normal(ks[0], (B, S, D), jnp.float32), 'gate_w': jax.random.normal(ks[1], (E, D), jnp.float32) * s, 'Wg': jax.random.normal(ks[2], (E, F_EXP, D), jnp.float32) * s, 'Wu': jax.random.normal(ks[3], (E, F_EXP, D), jnp.float32) * s, 'Wd': jax.random.normal(ks[4], (E, D, F_EXP), jnp.float32) * s, 'Ws_g': jax.random.normal(ks[5], (F_SH, D), jnp.float32) * s, 'Ws_u': jax.random.normal(ks[6], (F_SH, D), jnp.float32) * s, 'Ws_d': jax.random.normal(ks[7], (D, F_SH), jnp.float32) * s}
    _L0_ffn_in = _L0_ffn_setup()
    _L0_c = _w((lambda *s: np.random.randn(*s).astype(np.float32) * 0.05)(32, 256))
    _L0_wmod = _w((lambda *s: np.random.randn(*s).astype(np.float32) * 0.05)(256, 6 * 256) * 256 ** (-0.5))
    _d = {'L0_attn_Q': _L0_attn_in['Q'], 'L0_attn_rot_w': _L0_attn_in['rot_w'], 'L0_attn_scale': _L0_attn_in['scale'], 'L0_attn_bias': _L0_attn_in['bias'], 'L0_ffn_gate_w': _L0_ffn_in['gate_w'], 'L0_ffn_Wg': _L0_ffn_in['Wg'], 'L0_ffn_Wu': _L0_ffn_in['Wu'], 'L0_ffn_Wd': _L0_ffn_in['Wd'], 'L0_ffn_Ws_g': _L0_ffn_in['Ws_g'], 'L0_ffn_Ws_u': _L0_ffn_in['Ws_u'], 'L0_ffn_Ws_d': _L0_ffn_in['Ws_d'], 'L0_c': _L0_c, 'L0_wmod': _L0_wmod}
    _x0 = _d['L0_attn_Q']
    _d['L0_attn_Q'] = jax.random.normal(jax.random.fold_in(jax.random.key(seed), 1), (32, 512, 256), dtype=_x0.dtype)
    del _x0
    return _d

def reference(L0_attn_Q, L0_attn_rot_w, L0_attn_scale, L0_attn_bias, L0_ffn_gate_w, L0_ffn_Wg, L0_ffn_Wu, L0_ffn_Wd, L0_ffn_Ws_g, L0_ffn_Ws_u, L0_ffn_Ws_d, L0_c, L0_wmod):

    def _L0_attn_ref(Q, rot_w, scale, bias):
        import jax, jax.numpy as jnp
        import numpy as np
        B, S, D = (4, 512, 256)

        def givens_rotate(r, x):
            g = r.reshape(-1, 2)
            g = g / jnp.linalg.norm(g, axis=-1, keepdims=True)
            xp = x.reshape(x.shape[:-1] + (x.shape[-1] // 2, 2))
            c, s = (g[:, 0], g[:, 1])
            y0 = c * xp[..., 0] - s * xp[..., 1]
            y1 = c * xp[..., 1] + s * xp[..., 0]
            return jnp.stack([y0, y1], axis=-1).reshape(x.shape)
        q = givens_rotate(rot_w[0], Q)
        k = givens_rotate(rot_w[1], Q)
        v = givens_rotate(rot_w[2], Q)
        zeros = jnp.zeros(Q.shape[:-1] + (1,), Q.dtype)
        q = jnp.concatenate([zeros, q], axis=-1)[:, None]
        k = jnp.concatenate([zeros, k], axis=-1)[:, None]
        v = jnp.concatenate([zeros, v], axis=-1)[:, None]
        sgn = jnp.concatenate([-jnp.ones((1,), Q.dtype), jnp.ones((q.shape[-1] - 1,), Q.dtype)])
        cin = jnp.einsum('bhqd,bhkd->bhqk', q * sgn, k)
        attn = jax.nn.softmax((2.0 + 2.0 * cin) / scale + bias, axis=-1)
        ave = jnp.einsum('bhqk,bhkd->bhqd', attn, v)
        inner = jnp.sum(ave * ave * sgn, axis=-1, keepdims=True)
        denom = jnp.sqrt(jnp.clip(jnp.abs(inner), 1e-08, None))
        out = (ave / denom)[:, 0]
        return out[..., 1:]

    def _L0_ffn_ref(hidden_states, gate_w, Wg, Wu, Wd, Ws_g, Ws_u, Ws_d):
        import jax, jax.numpy as jnp
        import numpy as np
        B, S, D = (4, 1024, 256)
        E, F_EXP = (16, 512)
        F_C = 2.0
        F_SH = 512
        b, s, d = hidden_states.shape
        e = gate_w.shape[0]
        cap = int(s * F_C / e)
        logits = jnp.einsum('bsd,ed->bse', hidden_states, gate_w)
        scores = jax.nn.softmax(logits, axis=-1).transpose(0, 2, 1)
        topk_w, topk_idx = jax.lax.top_k(scores, cap)
        x_tok = jnp.take_along_axis(hidden_states[:, None, :, :], topk_idx[..., None], axis=2)
        g = jnp.einsum('becd,efd->becf', x_tok, Wg)
        u = jnp.einsum('becd,efd->becf', x_tok, Wu)
        h = jax.nn.gelu(g, approximate=False) * u
        eo = jnp.einsum('becf,edf->becd', h, Wd) * topk_w[..., None]
        offs = (jnp.arange(b) * s)[:, None, None]
        flat_idx = (topk_idx + offs).reshape(-1)
        flat = jnp.zeros((b * s, d), hidden_states.dtype)
        flat = flat.at[flat_idx].add(eo.reshape(-1, d))
        out = flat.reshape(b, s, d)
        gs = jnp.einsum('bsd,fd->bsf', hidden_states, Ws_g)
        us = jnp.einsum('bsd,fd->bsf', hidden_states, Ws_u)
        shared = jnp.einsum('bsf,df->bsd', jax.nn.gelu(gs, approximate=False) * us, Ws_d)
        return out + shared
    x = L0_attn_Q
    mod = (_silu(L0_c) @ L0_wmod).reshape(L0_c.shape[0], 6, 1, -1)
    sa, ca, ga, sb, cb, gb = (mod[:, 0], mod[:, 1], mod[:, 2], mod[:, 3], mod[:, 4], mod[:, 5])
    ga = (2 * (ga >= 0) - 1) * jnp.maximum(jnp.abs(ga), 0.25)
    gb = (2 * (gb >= 0) - 1) * jnp.maximum(jnp.abs(gb), 0.25)
    h = _layernorm(x, axis=-1) * (1 + ca) + sa
    x = x + ga * _L0_attn_ref(h, L0_attn_rot_w, L0_attn_scale, L0_attn_bias)
    h = _layernorm(x, axis=-1) * (1 + cb) + sb
    x = x + gb * _L0_ffn_ref(h, L0_ffn_gate_w, L0_ffn_Wg, L0_ffn_Wu, L0_ffn_Wd, L0_ffn_Ws_g, L0_ffn_Ws_u, L0_ffn_Ws_d)
    return x

_drawn_inputs = setup_inputs


def setup_inputs(seed=0):
    import zlib

    import numpy as np

    out = dict(_drawn_inputs(seed))
    spreads = {}
    factors = {'L0_attn_rot_w': 3.625,
     'L0_ffn_gate_w': 8.0,
     'L0_ffn_Wg': 8.0,
     'L0_ffn_Wu': 8.0,
     'L0_ffn_Wd': 8.0,
     'L0_ffn_Ws_g': 8.0,
     'L0_ffn_Ws_u': 8.0,
     'L0_ffn_Ws_d': 8.0,
     'L0_c': 3.341,
     'L0_wmod': 3.314}
    for name, (base, spread) in spreads.items():
        noise = np.random.default_rng([zlib.crc32(name.encode()), seed]).standard_normal(out[name].shape)
        drawn = base * np.exp(spread * noise) if base else spread * noise
        out[name] = jnp.asarray(drawn.astype(out[name].dtype))
    for name, factor in factors.items():
        out[name] = (out[name] * factor).astype(out[name].dtype)
    return out
```

```python
from contextlib import ExitStack

import concourse.bass as bass
from concourse import mybir

ALU = mybir.AluOpType
ACT = mybir.ActivationFunctionType
AX = mybir.AxisListType
F32 = mybir.dt.float32
F32R = mybir.dt.float32r
U32 = mybir.dt.uint32

P = 128
B, S, D = 32, 512, 256
E, F = 16, 512
CAP = S * 2 // E
T = S // P
KD = D // P
KF = F // P
GROUP = P // E
NG = B // GROUP
TT = GROUP * CAP // P
WCOLS = KD * F
NMOD = 4
GA, SB, CB, GB = range(NMOD)
EPS = 1e-5
HI, LO = 0, 1
C_ID, C_SWAP = 0, P
C_EVEN, C_ODD, C_SIGN, C_BASE, C_HALF = range(2 * P, 2 * P + 5)
C_ALL = C_HALF + max(T, 3 * KD)


def block_kernel(nc, x, rot, scale, bias, gate_t, w_exp, w_sh, c, wmod, consts, out):
    h2_dram = nc.dram_tensor("h2_rows", (B * S, D), F32).ap()
    mod_dram = nc.dram_tensor("mod_rows", (B, NMOD * D), F32).ap()
    x_v = x.rearrange("b (p t) d -> b p (t d)", t=T)
    out_v = out.rearrange("b (p t) d -> b p (t d)", t=T)
    out_rows = out.rearrange("b s d -> (b s) d")
    h2_v = h2_dram.rearrange("(b p t) d -> b p (t d)", b=B, t=T)

    with ExitStack() as ctx:
        def sb(name, shape, dt=F32):
            return ctx.enter_context(nc.sbuf_tensor(name, shape, dt))

        def sem(name):
            return ctx.enter_context(nc.semaphore(name))

        W = [sb(f"weights{j}", [P, 2, 3 * WCOLS], F32R) for j in range(2)]
        XT = [sb(f"x_t{j}", [P, 2, KD, S], F32R) for j in range(2)]
        H = [sb(f"hidden{j}", [P, 2, KF, S], F32R) for j in range(2)]
        K_T = sb("k_t", [P, 2, KD, S], F32R)
        V = sb("v", [P, 2, T, D], F32R)
        ROTK = sb("rot_k", [P, 2, KD, P], F32R)
        ROTV = sb("rot_v", [P, 2, KD, P], F32R)
        GW = sb("gate_w", [P, 2, KD, E], F32R)
        H1_T, H2_T = XT
        HID = H[0]
        A_T = H[1]

        X = sb("x_rows", [P, 2, T * D])
        X1 = sb("x1_rows", [P, 2, T * D])
        PAIRS = sb("pairs", [P, B // 2, D])
        STAGE = sb("stage", [P, 3 * WCOLS])
        TMP = sb("tmp_rows", [P, T, D])
        Y = sb("y_rows", [P, T, D])
        GEL = sb("gelu", [P, 2, S])
        HM = sb("hidden_f32", [P, 2, S])
        SG = sb("scores", [P, T, B, E])
        SQ = sb("squares", [P, D])
        ROW = [sb(f"score_rows{j}", [P, S]) for j in range(2)]
        CONST = sb("consts", [P, C_ALL])
        pairs_flat = PAIRS[:, :, :].rearrange("p a d -> p (a d)")
        EXPS = pairs_flat[:, 0:T * S].rearrange("p (t s) -> p t s", t=T)
        MODB = pairs_flat[:, T * S:].rearrange("p (j m d) -> p j m d", j=2, m=NMOD)
        WMOD = pairs_flat[:, 0:KD * 6 * D].rearrange("p (k n) -> p k n", k=KD)
        XN = STAGE[:, 0:T * D].rearrange("p (t d) -> p t d", t=T)
        H2 = STAGE[:, T * D:2 * T * D].rearrange("p (t d) -> p t d", t=T)
        H1_F = STAGE[:, 2 * T * D:].rearrange("p (k s) -> p k s", k=KD)
        mods = X1[:, :, :].rearrange("p j n -> p (j n)")[0:B, 0:6 * D]

        ROT = sb("rot_raw", [P, 3, KD])
        ROT_SW = sb("rot_swapped", [P, 3, KD])
        COS = sb("cosines", [P, 3, KD])
        SIN = sb("sines", [P, 3, KD])
        RN = sb("rot_norm", [P, 3, KD])
        CS = sb("k_cos_sin", [P, 4, KD])
        ROTF = sb("rot_f32", [P, 2, KD, P])
        SCB = sb("scale_bias", [P, 8])
        GWF = sb("gate_f32", [P, KD, E])
        CIN = sb("cond", [B, D])
        CACT = sb("cond_silu", [B, D])
        CACT_T = sb("cond_t", [P, KD, B])
        SGNS = sb("mod_signs", [B, 3, D])
        SACA = sb("sa_ca_t", [P, 2, KD, B])
        ST = [sb(f"bn_stats{j}", [P, T, 6]) for j in range(2)]
        MV = [sb(f"mean_var{j}", [P, T, 2]) for j in range(2)]
        RS = [sb(f"rstd{j}", [P, T]) for j in range(2)]
        NM = sb("neg_max", [P, T])
        NB = sb("exp_bias", [P, T])
        Z = sb("exp_sum", [P, T])
        ZZ = sb("exp_sum_sq", [P, T])
        SSQ = sb("sum_squares", [P, T])
        NSQ = sb("norm_squares", [P, T])
        FAC = sb("out_factor", [P, T])
        GMX = sb("gate_max", [P, T])
        GLT = sb("gate_logits_t", [E, S])
        GL = sb("gate_logits", [P, T, E])
        GEX = sb("gate_exp", [P, T, E])
        GS = sb("gate_sum", [P, T])
        GR = sb("gate_rsum", [P, T])
        TOPV = sb("top_values", [P, 2, CAP])
        TOPU = sb("top_positions", [P, CAP], U32)
        TOPI = sb("top_indices", [P, 2, CAP])
        IDX = sb("slot_token", [P, E, NG * TT], U32)
        WGT = sb("slot_weight", [P, E, NG * TT])
        ICUR = [sb(f"step_token{j}", [P, TT], U32) for j in range(4)]
        WCUR = [sb(f"step_weight{j}", [P, TT]) for j in range(4)]

        PS = ctx.enter_context(nc.psum_tensor("ps", [P, 4096], F32))
        PC, PD, PG = PS[:, 0:2048], PS[:, 2048:3072], PS[:, 3072:4096]

        IDENT = CONST[:, C_ID:C_ID + P]
        SWAP = CONST[:, C_SWAP:C_SWAP + P]

        def const(j, n=1):
            return CONST[:, j:j + n]

        consts_in, rot_in, cond_in, wmod_in, gate_in, scal_in = map(
            sem, ("consts_in", "rot_in", "cond_in", "wmod_in", "gate_in", "scal_in"))
        w_in = sem("w_in")
        dve_setup, rot_sw_ps, rot_sq, rot_rn, silu_done, cond_t_ps, cond_t, mods_ps = map(
            sem, ("dve_setup", "rot_sw_ps", "rot_sq", "rot_rn", "silu_done", "cond_t_ps", "cond_t", "mods_ps"))
        mods_ready, mods_t_ps, setup_done, mods_stored = map(
            sem, ("mods_ready", "mods_t_ps", "setup_done", "mods_stored"))
        w_hi, w_lo = sem("w_hi"), sem("w_lo")
        x_in = [sem("x_in0"), sem("x_in1")]
        mod_in = [sem("mod_in0"), sem("mod_in1")]
        st1, mv1, ve1, rs1, xn_ready = map(sem, ("st1", "mv1", "ve1", "rs1", "xn_ready"))
        xt_done, h1f_ready, h1_hi, h1_lo = map(sem, ("xt_done", "h1f_ready", "h1_hi", "h1_lo"))
        k_done, k_hi, k_lo, v_done, v_hi, v_lo = map(sem, ("k_done", "k_hi", "k_lo", "v_done", "v_hi", "v_lo"))
        s_done, nmax, ebias, exp_done = map(sem, ("s_done", "nmax", "ebias", "exp_done"))
        at_done, at_hi, at_lo, av_done = map(sem, ("at_done", "at_hi", "at_lo", "av_done"))
        ssq_done, zz_ready, norm_sq, fac_ready, u_read, x1_ready = map(
            sem, ("ssq_done", "zz_ready", "norm_sq", "fac_ready", "u_read", "x1_ready"))
        st2, mv2, ve2, rs2, cent2, h2_ready, h2_stored = map(
            sem, ("st2", "mv2", "ve2", "rs2", "cent2", "h2_ready", "h2_stored"))
        h2t_done, h2t_hi, h2t_lo = map(sem, ("h2t_done", "h2t_hi", "h2t_lo"))
        gate_done, gate_read, gate_t_done, gmax_ready, gl_ready, gexp_done, gsum, grs, sg_ready = map(
            sem, ("gate_done", "gate_read", "gate_t_done", "gmax_ready", "gl_ready", "gexp_done", "gsum", "grs", "sg_ready"))
        gu_done, gelu_done, mul_done, hid_hi, hid_lo = map(
            sem, ("gu_done", "gelu_done", "mul_done", "hid_hi", "hid_lo"))
        down_done, y_read, y_ready, y_stored = map(sem, ("down_done", "y_read", "y_ready", "y_stored"))
        pairs_in, sgt_ps, row_ready, top_step, tops_ready, tops_t_ps, tops_read, slots_ready = map(
            sem, ("pairs_in", "sgt_ps", "row_ready", "top_step", "tops_ready", "tops_t_ps", "tops_read",
                  "slots_ready"))
        cur_ready = sem("cur_ready")
        gathered = [sem(f"gathered{j}") for j in range(2)]
        tx_done, tx_hi, tx_lo = map(sem, ("tx_done", "tx_hi", "tx_lo"))
        egu_done, egelu_done, emul_done, ehid_hi, ehid_lo, edown_done, eo_ready = map(
            sem, ("egu_done", "egelu_done", "emul_done", "ehid_hi", "ehid_lo", "edown_done", "eo_ready"))
        scattered = [sem(f"scattered{j}") for j in range(NG)]

        def valid(n):
            return not isinstance(n, int) or 0 <= n < B

        def wait(e, s, count):
            if not isinstance(count, int) or count > 0:
                e.wait_ge(s, count)

        def wait_apart(e, s, count):
            if not isinstance(count, int):
                e.compute_val(count)
            e.wait_ge(consts_in, 16)
            wait(e, s, count)

        def phase_a(e, iteration):
            for i in (-1, 0, 1, 2):
                iteration(i, i % 2, i // 2)
            with e.Fori(1, (B - 2) // 2) as half:
                iteration(half * 2 + 1, 1, half)
                iteration(half * 2 + 2, 0, half + 1)
            for i in (B - 1, B, B + 1):
                iteration(i, i % 2, i // 2)

        def phase_b(e, step):
            for g in range(NG):
                step(0, 0, g, first=g == 0)
            with e.Fori(0, (E - 2) // 2) as ii:
                for j in (1, 2):
                    for g in range(NG):
                        step(ii * 2 + j, j % 2, g)
            for g in range(NG):
                step(E - 1, (E - 1) % 2, g, last=g == NG - 1)

        def wg(j, part, k, fc):
            return W[j][:, part, k * F + fc * P:k * F + fc * P + P]

        def wu(j, part, k, fc):
            return W[j][:, part, WCOLS + k * F + fc * P:WCOLS + k * F + fc * P + P]

        def wd(j, part, fc):
            return W[j][:, part, 2 * WCOLS + fc * D:2 * WCOLS + fc * D + D]

        block = ctx.enter_context(nc.Block())

        @block.sync
        def _(sp):
            sp.dma_start(CONST[:, :], consts).then_inc(consts_in, 16)
            sp.dma_start(ROT[:, :, :].rearrange("p a k -> p (a k)"), rot).then_inc(rot_in, 16)
            sp.dma_start(SCB[:, 0:1], scale.to_broadcast((P, 1))).then_inc(scal_in, 16)
            sp.dma_start(SCB[:, 1:2], bias.to_broadcast((P, 1))).then_inc(scal_in, 16)
            sp.dma_start(CIN[:, :], c).then_inc(cond_in, 16)
            sp.dma_start(WMOD, wmod.rearrange("(k p) n -> p k n", p=P)).then_inc(wmod_in, 16)
            sp.dma_start(GWF[:, :, :].rearrange("p k e -> p (k e)"), gate_t).then_inc(gate_in, 16)
            sp.dma_start(X[:, 0, :], x_v[0]).then_inc(x_in[0], 16)
            for m in range(3):
                sp.dma_start(STAGE[:, m * WCOLS:(m + 1) * WCOLS], w_sh[m]).then_inc(w_in, 16)
            sp.wait_ge(w_hi, 1)
            sp.wait_ge(w_lo, 1)
            for m in range(3):
                sp.dma_start(STAGE[:, m * WCOLS:(m + 1) * WCOLS], w_exp[m][0]).then_inc(w_in, 16)
            sp.wait_ge(mods_ready, 1)
            sp.dma_start(mod_dram, mods[:, 2 * D:]).then_inc(mods_stored, 16)
            sp.wait_ge(mods_stored, 16)

            def iteration(i, p, half):
                if valid(i + 1) and not (isinstance(i, int) and i < 0):
                    wait(sp, x1_ready, i)
                    sp.dma_start(X[:, 1 - p, :], x_v[i + 1]).then_inc(x_in[1 - p], 16)
                if valid(i - 1):
                    wait(sp, h2_ready, i)
                    sp.dma_start(h2_v[i - 1], H2.rearrange("p t d -> p (t d)")).then_inc(h2_stored, 16)
                if valid(i - 2):
                    wait(sp, y_ready, i - 1)
                    sp.dma_start(out_v[i - 2], Y[:, :, :].rearrange("p t d -> p (t d)")).then_inc(y_stored, 16)
                if valid(i):
                    wait(sp, y_read, (i - 1))
                    sp.dma_start(MODB[:, p, :, :].rearrange("p m d -> p (m d)"),
                                 mod_dram[bass.ds(i, 1), :].to_broadcast((P, NMOD * D))).then_inc(mod_in[p], 16)

            phase_a(sp, iteration)

            sp.wait_ge(exp_done, T * B)
            sp.wait_ge(at_done, T * B)
            sp.wait_ge(y_read, B)
            for half in range(2):
                gb = mod_dram.rearrange("(a h) (m d) -> h m a d", h=2, m=NMOD)[half, GB]
                sp.dma_start(PAIRS[half * CAP:(half + 1) * CAP, :, :],
                             gb.unsqueeze(0).to_broadcast((CAP, B // 2, D))).then_inc(pairs_in, 16)
            sp.wait_ge(h2_stored, 16 * B)
            sp.wait_ge(h2t_done, KD * B)

            def step(e, p, g, first=False, last=False):
                if g == 0 and not (isinstance(e, int) and e == E - 1):
                    sp.wait_ge(w_hi, e * 3 + 4)
                    sp.wait_ge(w_lo, e * 3 + 4)
                    for m in range(3):
                        sp.dma_start(STAGE[:, m * WCOLS:(m + 1) * WCOLS], w_exp[m][e + 1]).then_inc(w_in, 16)

            phase_b(sp, step)
            sp.wait_ge(y_stored, 16 * B)

        @block.tensor
        def _(pe):
            def mm3(o, lhs, rhs, start, stop):
                pe.matmul(o, lhs(HI), rhs(HI), start=start, stop=False)
                pe.matmul(o, lhs(HI), rhs(LO), start=False, stop=False)
                return pe.matmul(o, lhs(LO), rhs(HI), start=False, stop=stop)

            pe.wait_ge(consts_in, 16)
            pe.wait_ge(rot_in, 16)
            pe.matmul(PG[:, 0:3 * KD], SWAP, ROT[:, :, :].rearrange("p a k -> p (a k)"),
                      start=True, stop=True).then_inc(rot_sw_ps, 1)
            pe.wait_ge(silu_done, 1)
            for k in range(KD):
                mm = pe.transpose(PG[:, 512 + k * B:512 + (k + 1) * B], CACT[:, k * P:(k + 1) * P], IDENT[0:B, 0:B])
            mm.then_inc(cond_t_ps, 1)
            pe.wait_ge(cond_t, 1)
            pe.wait_ge(wmod_in, 16)
            for n in range(3):
                for k in range(KD):
                    mm = pe.matmul(PC[0:B, n * 512:(n + 1) * 512], CACT_T[:, k, :], WMOD[:, k, n * 512:(n + 1) * 512],
                                   start=k == 0, stop=k == KD - 1)
            mm.then_inc(mods_ps, 1)
            pe.wait_ge(mods_ready, 1)
            for j in range(2):
                for k in range(KD):
                    n = j * KD + k
                    mm = pe.transpose(PD[:, n * B:(n + 1) * B], mods[:, j * D + k * P:j * D + (k + 1) * P],
                                      IDENT[0:B, 0:B])
            mm.then_inc(mods_t_ps, 1)
            pe.wait_ge(setup_done, 1)

            def x_transposes(n):
                wait(pe, xn_ready, n + 1)
                wait(pe, at_hi, n * T)
                wait(pe, at_lo, n * T)
                for k in range(KD):
                    for t in range(T):
                        mm = pe.transpose(PC[:, k * S + t * P:k * S + (t + 1) * P], XN[:, t, k * P:(k + 1) * P], IDENT)
                mm.then_inc(xt_done, 1)

            def k_and_v(n):
                wait(pe, h1_hi, n + 1)
                wait(pe, h1_lo, n + 1)
                for k in range(KD):
                    mm = mm3(PC[:, (KD + k) * S:(KD + k + 1) * S], lambda a: ROTK[:, a, k, :],
                             lambda a: H1_T[:, a, k, :], True, True)
                mm.then_inc(k_done, 1)
                for t in range(T):
                    for k in range(KD):
                        mm = mm3(PC[:, t * D + k * P:t * D + (k + 1) * P],
                                 lambda a: H1_T[:, a, k, t * P:(t + 1) * P], lambda a: ROTV[:, a, k, :], True, True)
                mm.then_inc(v_done, 1)

            def scores(n):
                wait(pe, k_hi, n + 1)
                wait(pe, k_lo, n + 1)
                wait(pe, v_hi, n + 1)
                wait(pe, v_lo, n + 1)
                for t in range(T):
                    for k in range(KD):
                        mm = mm3(PC[:, t * S:(t + 1) * S], lambda a: H1_T[:, a, k, t * P:(t + 1) * P],
                                 lambda a: K_T[:, a, k, :], k == 0, k == KD - 1)
                    mm.then_inc(s_done, 1)

            def a_transposes(n):
                for t in range(T):
                    wait(pe, exp_done, n * T + t + 1)
                    for q in range(T):
                        mm = pe.transpose(PC[:, t * S + q * P:t * S + (q + 1) * P], EXPS[:, t, q * P:(q + 1) * P],
                                          IDENT)
                    mm.then_inc(at_done, 1)

            def a_times_v(n, half):
                for t in (2 * half, 2 * half + 1):
                    wait(pe, at_hi, n * T + t + 1)
                    wait(pe, at_lo, n * T + t + 1)
                    if t == 2:
                        wait(pe, gl_ready, n)
                    for q in range(T):
                        mm = mm3(PD[:, t * D:(t + 1) * D], lambda a: A_T[:, a, t, q * P:(q + 1) * P],
                                 lambda a: V[:, a, q, :], q == 0, q == T - 1)
                    mm.then_inc(av_done, 1)

            def h2_transposes(n):
                wait(pe, h2_ready, n + 1)
                wait(pe, mul_done, n * KF)
                for k in range(KD):
                    for t in range(T):
                        mm = pe.transpose(PG[:, k * S + t * P:k * S + (t + 1) * P], H2[:, t, k * P:(k + 1) * P], IDENT)
                    mm.then_inc(h2t_done, 1)

            def gate(n):
                wait(pe, y_read, n)
                for k in range(KD):
                    wait(pe, h2t_hi, n * KD + k + 1)
                    wait(pe, h2t_lo, n * KD + k + 1)
                    mm = mm3(PD[0:E, 512:512 + S], lambda a: GW[:, a, k, :], lambda a: H2_T[:, a, k, :],
                             k == 0, k == KD - 1)
                mm.then_inc(gate_done, 1)

            def gate_transposes(n):
                wait_apart(pe, gate_read, n + 1)
                for t in range(T):
                    mm = pe.transpose(PD[:, 512 + t * E:512 + (t + 1) * E], GLT[:, t * P:(t + 1) * P],
                                      IDENT[0:E, 0:E])
                mm.then_inc(gate_t_done, 1)

            def gate_up(n, fc):
                wait(pe, h2t_hi, (n + 1) * KD)
                wait(pe, h2t_lo, (n + 1) * KD)
                wait(pe, mul_done, n * KF + fc)
                for half, w in ((0, wg), (1, wu)):
                    for k in range(KD):
                        mm = mm3(PG[:, half * S:(half + 1) * S], lambda a: w(0, a, k, fc),
                                 lambda a: H2_T[:, a, k, :], k == 0, k == KD - 1)
                mm.then_inc(gu_done, 1)

            def down(n):
                wait(pe, u_read, min(n + 2, B) if isinstance(n, int) else n + 2)
                if isinstance(n, int) and n == B - 1:
                    wait(pe, gl_ready, B)
                for t in range(T):
                    for fc in range(KF):
                        if t == 0:
                            wait(pe, hid_hi, n * KF + fc + 1)
                            wait(pe, hid_lo, n * KF + fc + 1)
                        mm = mm3(PD[:, t * D:(t + 1) * D], lambda a: HID[:, a, fc, t * P:(t + 1) * P],
                                 lambda a: wd(0, a, fc), fc == 0, fc == KF - 1)
                mm.then_inc(down_done, 1)

            def iteration(i, p, half):
                if valid(i):
                    k_and_v(i)
                if valid(i - 2):
                    gate_up(i - 2, 3)
                if valid(i):
                    scores(i)
                if valid(i - 2):
                    down(i - 2)
                if valid(i - 1):
                    h2_transposes(i - 1)
                if valid(i):
                    a_transposes(i)
                if valid(i - 1):
                    gate(i - 1)
                    gate_up(i - 1, 0)
                    gate_transposes(i - 1)
                if valid(i):
                    a_times_v(i, 0)
                if valid(i + 1):
                    x_transposes(i + 1)
                if valid(i - 1):
                    gate_up(i - 1, 1)
                if valid(i):
                    a_times_v(i, 1)
                if valid(i - 1):
                    gate_up(i - 1, 2)

            phase_a(pe, iteration)

            pe.wait_ge(sg_ready, B)
            for g in range(NG):
                if g >= 1:
                    pe.wait_ge(row_ready, g)
                for t in range(T):
                    mm = pe.transpose(PC[:, t * P:(t + 1) * P],
                                      SG[:, t, g * GROUP:(g + 1) * GROUP, :].rearrange("p b e -> p (b e)"), IDENT)
                mm.then_inc(sgt_ps, 1)
                pe.wait_ge(tops_ready, g + 1)
                if g >= 1:
                    pe.wait_ge(tops_read, g)
                pe.transpose(PC[:, 512:512 + P], TOPI[:, :, :].rearrange("p h c -> p (h c)"), IDENT)
                pe.transpose(PC[:, 512 + P:512 + 2 * P], TOPV[:, :, :].rearrange("p h c -> p (h c)"),
                             IDENT).then_inc(tops_t_ps, 1)
            pe.wait_ge(y_read, B)
            pe.wait_ge(slots_ready, 1)

            def rows_transposes(e, g):
                s, p = e * NG + g, g % 2
                pe.wait_ge(gathered[p], (e * (NG // 2) + g // 2 + 1) * (TT * 16))
                wait(pe, tx_hi, s)
                wait(pe, tx_lo, s)
                for k in range(KD):
                    for t in range(TT):
                        mm = pe.transpose(PC[:, 1024 + k * S + t * P:1024 + k * S + (t + 1) * P],
                                          X[:, p, t * D + k * P:t * D + (k + 1) * P], IDENT)
                mm.then_inc(tx_done, 1)

            def e_gate_up(s, g, j, fc):
                if fc == 0:
                    pe.wait_ge(tx_hi, s + 1)
                    pe.wait_ge(tx_lo, s + 1)
                bank = PG if fc % 2 == 0 else PC[:, 0:1024]
                wait(pe, emul_done, s * KF + fc - 1)
                for half, w in ((0, wg), (1, wu)):
                    for k in range(KD):
                        mm = mm3(bank[:, half * S:(half + 1) * S], lambda a: w(j, a, k, fc),
                                 lambda a: XT[g % 2][:, a, k, :], k == 0, k == KD - 1)
                mm.then_inc(egu_done, 1)

            def e_down(s, g, j, tiles):
                for t in tiles:
                    for fc in range(KF):
                        if t == 0:
                            pe.wait_ge(ehid_hi, s * KF + fc + 1)
                            pe.wait_ge(ehid_lo, s * KF + fc + 1)
                        if fc == 0:
                            wait(pe, eo_ready, (s - 1) * TT + (t // 2 + 1) * 2)
                        mm = mm3(PD[:, t * D:(t + 1) * D], lambda a: H[g % 2][:, a, fc, t * P:(t + 1) * P],
                                 lambda a: wd(j, a, fc), fc == 0, fc == KF - 1)
                    mm.then_inc(edown_done, 1)

            def step(e, p, g, first=False, last=False):
                s = e * NG + g
                j = 1 - p
                jd = j if g else 1 - j
                if first:
                    rows_transposes(0, 0)
                if g == 0:
                    pe.wait_ge(w_hi, e * 3 + 4)
                    pe.wait_ge(w_lo, e * 3 + 4)
                e_gate_up(s, g, j, 0)
                if not first:
                    e_down(s - 1, g - 1, jd, (0, 1))
                e_gate_up(s, g, j, 1)
                if not first:
                    e_down(s - 1, g - 1, jd, (2, 3))
                e_gate_up(s, g, j, 2)
                if not last:
                    rows_transposes(e, g + 1)
                e_gate_up(s, g, j, 3)
                if last:
                    e_down(s, g, j, range(TT))

            phase_b(pe, step)

        @block.scalar
        def _(act):
            act.wait_ge(cond_in, 16)
            act.activation(CACT[:, :], CIN[:, :], ACT.Silu).then_inc(silu_done, 1)
            act.wait_ge(w_in, 48)
            act.copy(W[0][:, HI, :], STAGE[:, :]).then_inc(w_hi, 1)
            act.wait_ge(w_in, 96)
            act.copy(W[1][:, HI, :], STAGE[:, :]).then_inc(w_hi, 3)
            act.wait_ge(setup_done, 1)

            def h1_modulate(n):
                act.wait_ge(xt_done, n + 1)
                wait(act, h1_hi, n)
                wait(act, h1_lo, n)
                for k in range(KD):
                    last = act.activation(H1_F[:, k, :], PC[:, k * S:(k + 1) * S], ACT.Identity,
                                          bias=SACA[:, 0, k, bass.ds(n, 1)], scale=SACA[:, 1, k, bass.ds(n, 1)])
                last.then_inc(h1f_ready, 1)

            def hidden(n, fc):
                act.wait_ge(gu_done, n * KF + fc + 1)
                act.activation(GEL[:, fc % 2, :], PG[:, 0:S], ACT.Gelu).then_inc(gelu_done, 1)
                act.wait_ge(mul_done, n * KF + fc + 1)
                wait(act, down_done, n)
                act.copy(HID[:, HI, fc, :], HM[:, fc % 2, :]).then_inc(hid_hi, 1)

            def squares(n, tiles):
                for t in tiles:
                    act.wait_ge(av_done, n * T + (t // 2 + 1) * 2)
                    wait(act, ssq_done, n * T + t)
                    act.activation(SQ[:, :], PD[:, t * D:(t + 1) * D], ACT.Square,
                                   accum_out=SSQ[:, t:t + 1]).then_inc(ssq_done, 1)

            def iteration(i, p, half):
                if valid(i):
                    act.wait_ge(k_done, i + 1)
                    act.copy(K_T[:, HI, :, :].rearrange("p k s -> p (k s)"), PC[:, KD * S:]).then_inc(k_hi, 1)
                    act.wait_ge(v_done, i + 1)
                    act.copy(V[:, HI, :, :].rearrange("p t d -> p (t d)"), PC[:, 0:T * D]).then_inc(v_hi, 1)
                if valid(i - 2):
                    hidden(i - 2, 3)
                    act.wait_ge(gl_ready, i - 1)
                    wait(act, sg_ready, i - 2)
                    act.activation(GEX[:, :, :], GL[:, :, :], ACT.Exp).then_inc(gexp_done, 1)
                if valid(i):
                    for t in range(T):
                        act.wait_ge(ebias, i * T + t + 1)
                        act.activation(EXPS[:, t, :], PC[:, t * S:(t + 1) * S], ACT.Exp, bias=NB[:, t:t + 1],
                                       accum_out=Z[:, t:t + 1]).then_inc(exp_done, 1)
                if valid(i - 1):
                    for k in range(KD):
                        act.wait_ge(h2t_done, (i - 1) * KD + k + 1)
                        act.copy(H2_T[:, HI, k, :], PG[:, k * S:(k + 1) * S]).then_inc(h2t_hi, 1)
                if valid(i):
                    for t in range(T):
                        act.wait_ge(at_done, i * T + t + 1)
                        act.copy(A_T[:, HI, t, :], PC[:, t * S:(t + 1) * S]).then_inc(at_hi, 1)
                if valid(i - 1):
                    act.wait_ge(gate_done, i)
                    wait(act, gate_t_done, i - 1)
                    act.copy(GLT[:, :], PD[0:E, 512:512 + S]).then_inc(gate_read, 1)
                    hidden(i - 1, 0)
                if valid(i):
                    squares(i, (0, 1))
                if valid(i + 1):
                    h1_modulate(i + 1)
                if valid(i - 1):
                    hidden(i - 1, 1)
                if valid(i):
                    squares(i, (2, 3))
                if valid(i - 1):
                    hidden(i - 1, 2)

            phase_a(act, iteration)

            def rows_hi(s, p):
                act.wait_ge(tx_done, s + 1)
                act.copy(XT[p][:, HI, :, :].rearrange("p k s -> p (k s)"), PC[:, 1024:]).then_inc(tx_hi, 1)

            act.wait_ge(y_read, B)

            def step(e, p, g, first=False, last=False):
                s = e * NG + g
                if first:
                    rows_hi(0, 0)
                if g >= 1 and not (isinstance(e, int) and e == E - 1):
                    act.wait_ge(w_in, (e + 1) * 48 + 96)
                    wait(act, edown_done, e * (NG * TT))
                    act.copy(W[p][:, HI, (g - 1) * WCOLS:g * WCOLS],
                             STAGE[:, (g - 1) * WCOLS:g * WCOLS]).then_inc(w_hi, 1)
                for fc in range(KF):
                    bank = PG if fc % 2 == 0 else PC[:, 0:1024]
                    act.wait_ge(egu_done, s * KF + fc + 1)
                    act.activation(GEL[:, fc % 2, :], bank[:, 0:S], ACT.Gelu).then_inc(egelu_done, 1)
                    if fc == 2 and not last:
                        rows_hi(s + 1, (g + 1) % 2)
                    act.wait_ge(emul_done, s * KF + fc + 1)
                    act.copy(H[g % 2][:, HI, fc, :], HM[:, fc % 2, :]).then_inc(ehid_hi, 1)

            phase_b(act, step)

        @block.vector
        def _(dve):
            links = [0]

            def link(ins):
                links[0] += 1
                ins.then_inc(dve_setup, 1)
                dve.wait_ge(dve_setup, links[0])

            def split_lo(o, full, hi):
                return dve.tensor_tensor(o, full, hi.bitcast(F32), ALU.subtract)

            dve.wait_ge(rot_sw_ps, 1)
            dve.wait_ge(scal_in, 32)
            flat = "p a k -> p (a k)"
            raw, sw = ROT[:, :, :].rearrange(flat), ROT_SW[:, :, :].rearrange(flat)
            cos, sin, rn = (a[:, :, :].rearrange(flat) for a in (COS, SIN, RN))
            link(dve.tensor_copy(sw, PG[:, 0:3 * KD]))
            link(dve.tensor_scalar(cos, raw, const(C_EVEN), None, ALU.mult))
            link(dve.scalar_tensor_tensor(cos, sw, const(C_ODD), cos, ALU.mult, ALU.add))
            link(dve.tensor_scalar(sin, raw, const(C_ODD), None, ALU.mult))
            link(dve.scalar_tensor_tensor(sin, sw, const(C_EVEN), sin, ALU.mult, ALU.add))
            link(dve.tensor_tensor(raw, cos, cos, ALU.mult))
            link(dve.tensor_tensor(sw, sin, sin, ALU.mult))
            dve.tensor_tensor(rn, raw, sw, ALU.add).then_inc(rot_sq, 1)
            dve.wait_ge(cond_t_ps, 1)
            dve.tensor_copy(CACT_T[:, :, :].rearrange("p k b -> p (k b)"), PG[:, 512:512 + KD * B]).then_inc(cond_t, 1)
            dve.wait_ge(rot_rn, 1)
            link(dve.tensor_tensor(cos, cos, rn, ALU.mult))
            link(dve.tensor_tensor(sin, sin, rn, ALU.mult))
            r2, cz, ncz = SCB[:, 3:4], SCB[:, 4:5], SCB[:, 5:6]
            link(dve.reciprocal(SCB[:, 2:3], SCB[:, 0:1]))
            link(dve.tensor_scalar(r2, SCB[:, 2:3], 2.0, None, ALU.mult))
            link(dve.tensor_tensor(cz, r2, SCB[:, 1:2], ALU.add))
            link(dve.tensor_scalar(ncz, cz, -1.0, None, ALU.mult))
            link(dve.tensor_tensor(CS[:, 0, :], COS[:, 0, :], COS[:, 1, :], ALU.mult))
            link(dve.tensor_tensor(CS[:, 1, :], SIN[:, 0, :], SIN[:, 1, :], ALU.mult))
            link(dve.tensor_tensor(CS[:, 2, :], COS[:, 0, :], SIN[:, 1, :], ALU.mult))
            link(dve.tensor_tensor(CS[:, 3, :], SIN[:, 0, :], COS[:, 1, :], ALU.mult))
            link(dve.tensor_tensor(CS[:, 0, :], CS[:, 0, :], CS[:, 1, :], ALU.add))
            link(dve.tensor_tensor(CS[:, 2, :], CS[:, 2, :], CS[:, 3, :], ALU.subtract))
            link(dve.tensor_scalar(CS[:, 0, :], CS[:, 0, :], r2, None, ALU.mult))
            link(dve.tensor_scalar(CS[:, 2, :], CS[:, 2, :], r2, const(C_SIGN), ALU.mult, ALU.mult))
            link(dve.tensor_scalar(CS[:, 3, :], SIN[:, 2, :], const(C_SIGN), None, ALU.mult))
            for m, (cc, ss, dst) in enumerate(((CS[:, 0, :], CS[:, 2, :], ROTK), (COS[:, 2, :], CS[:, 3, :], ROTV))):
                for k in range(KD):
                    link(dve.tensor_scalar(ROTF[:, m, k, :], IDENT, cc[:, k:k + 1], None, ALU.mult))
                    link(dve.scalar_tensor_tensor(ROTF[:, m, k, :], SWAP, ss[:, k:k + 1], ROTF[:, m, k, :],
                                                  ALU.mult, ALU.add))
                link(dve.tensor_copy(dst[:, HI, :, :], ROTF[:, m, :, :]))
                link(split_lo(dst[:, LO, :, :], ROTF[:, m, :, :], dst[:, HI, :, :]))
            dve.wait_ge(gate_in, 16)
            link(dve.tensor_copy(GW[:, HI, :, :], GWF[:, :, :]))
            link(split_lo(GW[:, LO, :, :], GWF[:, :, :], GW[:, HI, :, :]))
            dve.wait_ge(mods_ps, 1)
            link(dve.tensor_copy(mods, PC[0:B, 0:6 * D]))
            for j in (1, 4):
                link(dve.tensor_scalar(mods[:, j * D:(j + 1) * D], mods[:, j * D:(j + 1) * D], 1.0, None, ALU.add))
            for j in (2, 5):
                g = mods[:, j * D:(j + 1) * D]
                link(dve.tensor_scalar(SGNS[:, 0, :], g, 0.0, 2.0, ALU.is_ge, ALU.mult))
                link(dve.tensor_scalar(SGNS[:, 0, :], SGNS[:, 0, :], 1.0, None, ALU.subtract))
                link(dve.tensor_scalar(SGNS[:, 1, :], g, -1.0, None, ALU.mult))
                link(dve.tensor_tensor(SGNS[:, 2, :], g, SGNS[:, 1, :], ALU.max))
                link(dve.scalar_tensor_tensor(g, SGNS[:, 2, :], 0.25, SGNS[:, 0, :], ALU.max, ALU.mult))
            dve.engine_nop().then_inc(mods_ready, 1)
            dve.wait_ge(mods_t_ps, 1)
            link(dve.tensor_copy(SACA[:, :, :, :].rearrange("p j k b -> p (j k b)"), PD[:, 0:2 * KD * B]))
            for j, n in ((0, 1), (1, 3)):
                dve.wait_ge(w_hi, 1 if j == 0 else 4)
                split_lo(W[j][:, LO, :], STAGE[:, :], W[j][:, HI, :]).then_inc(w_lo, n)
            dve.wait_ge(w_lo, 4)
            dve.engine_nop().then_inc(setup_done, 1)

            def row_stats(rows, j, st, mv, n):
                for t in range(T):
                    last = dve.bn_stats(ST[j][:, t, :], rows(t))
                last.then_inc(st, 1)
                wait_apart(dve, st, n + 1)
                for t in range(T):
                    last = dve.bn_aggr(MV[j][:, t, :], ST[j][:, t, :])
                last.then_inc(mv, 1)

            def ln1_stats(n, p, loads):
                dve.wait_ge(x_in[p], loads * 16)
                row_stats(lambda t: X[:, p, t * D:(t + 1) * D], 0, st1, mv1, n)

            def ln1_apply(n, p):
                dve.wait_ge(rs1, n + 1)
                wait(dve, xt_done, n)
                for t in range(T):
                    last = dve.tensor_scalar(XN[:, t, :], X[:, p, t * D:(t + 1) * D], MV[0][:, t, 0:1],
                                             RS[0][:, t:t + 1], ALU.subtract, ALU.mult)
                last.then_inc(xn_ready, 1)

            def h1_split(n):
                dve.wait_ge(h1f_ready, n + 1)
                dve.tensor_copy(H1_T[:, HI, :, :], H1_F).then_inc(h1_hi, 1)
                dve.wait_ge(h1_hi, n + 1)
                split_lo(H1_T[:, LO, :, :], H1_F, H1_T[:, HI, :, :]).then_inc(h1_lo, 1)

            def hidden(n, fc):
                dve.wait_ge(gelu_done, n * KF + fc + 1)
                wait(dve, hid_hi, n * KF + fc - 1)
                wait(dve, hid_lo, n * KF + fc - 1)
                dve.tensor_tensor(HM[:, fc % 2, :], GEL[:, fc % 2, :], PG[:, S:], ALU.mult).then_inc(mul_done, 1)

            def out_norm(n):
                dve.scalar_tensor_tensor(ZZ[:, :], Z[:, :], 1e-8, Z[:, :], ALU.mult, ALU.mult).then_inc(zz_ready, 1)
                dve.wait_ge(zz_ready, n + 1)
                dve.wait_ge(ssq_done, (n + 1) * T)
                dve.tensor_tensor(NSQ[:, :], ZZ[:, :], SSQ[:, :], ALU.max).then_inc(norm_sq, 1)

            def attention_out(n, p, loads):
                dve.wait_ge(mod_in[p], loads * 16)
                dve.wait_ge(fac_ready, n + 1)
                for t in range(T):
                    last = dve.scalar_tensor_tensor(TMP[:, t, :], PD[:, t * D:(t + 1) * D], FAC[:, t:t + 1],
                                                    MODB[:, p, GA, :], ALU.mult, ALU.mult)
                last.then_inc(u_read, 1)

            def ln2_stats(n, p):
                dve.wait_ge(x1_ready, n + 1)
                row_stats(lambda t: X1[:, p, t * D:(t + 1) * D], 1, st2, mv2, n)

            def ln2_centre(n, p):
                dve.wait_ge(mv2, n + 1)
                for t in range(T):
                    last = dve.scalar_tensor_tensor(TMP[:, t, :], X1[:, p, t * D:(t + 1) * D], MV[1][:, t, 0:1],
                                                    MODB[:, p, CB, :], ALU.subtract, ALU.mult)
                last.then_inc(cent2, 1)

            def ln2_apply(n, p):
                dve.wait_ge(cent2, n + 1)
                dve.wait_ge(rs2, n + 1)
                wait(dve, h2t_done, n * KD)
                wait(dve, h2_stored, n * 16)
                for t in range(T):
                    last = dve.scalar_tensor_tensor(H2[:, t, :], TMP[:, t, :], RS[1][:, t:t + 1],
                                                    MODB[:, p, SB, :], ALU.mult, ALU.add)
                last.then_inc(h2_ready, 1)

            def score_max(n, tiles):
                for t in tiles:
                    dve.wait_ge(s_done, n * T + t + 1)
                    dve.tensor_reduce(NM[:, t:t + 1], PC[:, t * S:(t + 1) * S], AX.X, ALU.max,
                                      negate=True).then_inc(nmax, 1)
                dve.wait_ge(nmax, n * T + t + 1)
                both = slice(tiles[0], tiles[1] + 1)
                dve.tensor_scalar(NB[:, both], NM[:, both], SCB[:, 5:6], SCB[:, 4:5], ALU.add,
                                  ALU.add).then_inc(ebias, 2)

            def gate_max(n):
                dve.wait_ge(gate_t_done, n + 1)
                logits = PD[:, 512:512 + T * E].rearrange("p (t e) -> p t e", t=T)
                dve.tensor_reduce(GMX[:, :], logits, AX.X, ALU.max).then_inc(gmax_ready, 1)
                dve.wait_ge(gmax_ready, n + 1)
                dve.tensor_tensor(GL[:, :, :], logits, GMX[:, :].unsqueeze(2).to_broadcast((P, T, E)),
                                  ALU.subtract).then_inc(gl_ready, 1)

            def gate_scores(n):
                dve.wait_ge(gexp_done, n + 1)
                dve.tensor_reduce(GS[:, :], GEX[:, :, :], AX.X, ALU.add).then_inc(gsum, 1)
                dve.wait_ge(gsum, n + 1)
                dve.reciprocal(GR[:, :], GS[:, :]).then_inc(grs, 1)
                dve.wait_ge(grs, n + 1)
                dve.tensor_tensor(SG[:, :, bass.ds(n, 1), :].rearrange("p t b e -> p t (b e)"), GEX[:, :, :],
                                  GR[:, :].unsqueeze(2).to_broadcast((P, T, E)), ALU.mult).then_inc(sg_ready, 1)

            def iteration(i, p, half):
                if valid(i - 1):
                    attention_out(i - 1, 1 - p, half + p)
                if valid(i):
                    dve.wait_ge(k_hi, i + 1)
                    split_lo(K_T[:, LO, :, :].rearrange("p k s -> p (k s)"), PC[:, KD * S:],
                             K_T[:, HI, :, :].rearrange("p k s -> p (k s)")).then_inc(k_lo, 1)
                    dve.wait_ge(v_hi, i + 1)
                    split_lo(V[:, LO, :, :].rearrange("p t d -> p (t d)"), PC[:, 0:T * D],
                             V[:, HI, :, :].rearrange("p t d -> p (t d)")).then_inc(v_lo, 1)
                if valid(i - 2):
                    hidden(i - 2, 3)
                if valid(i - 1):
                    ln2_stats(i - 1, 1 - p)
                if valid(i):
                    score_max(i, (0, 1))
                if valid(i - 1):
                    ln2_centre(i - 1, 1 - p)
                if valid(i):
                    score_max(i, (2, 3))
                if valid(i - 1):
                    ln2_apply(i - 1, 1 - p)
                if valid(i + 1):
                    ln1_stats(i + 1, 1 - p, half + 1 + p)
                if valid(i - 2):
                    dve.wait_ge(down_done, i - 1)
                    wait(dve, y_stored, (i - 2) * 16)
                    dve.tensor_tensor(Y[:, :, :], PD.rearrange("p (t d) -> p t d", t=T),
                                      MODB[:, p, GB, :].unsqueeze(1).to_broadcast((P, T, D)),
                                      ALU.mult).then_inc(y_read, 1)
                if valid(i - 1):
                    for k in range(KD):
                        dve.wait_ge(h2t_hi, (i - 1) * KD + k + 1)
                        split_lo(H2_T[:, LO, k, :], PG[:, k * S:(k + 1) * S], H2_T[:, HI, k, :]).then_inc(h2t_lo, 1)
                if valid(i):
                    for t in range(T):
                        dve.wait_ge(at_hi, i * T + t + 1)
                        split_lo(A_T[:, LO, t, :], PC[:, t * S:(t + 1) * S], A_T[:, HI, t, :]).then_inc(at_lo, 1)
                if valid(i + 1):
                    ln1_apply(i + 1, 1 - p)
                if valid(i - 2):
                    gate_scores(i - 2)
                if valid(i - 1):
                    gate_max(i - 1)
                    hidden(i - 1, 0)
                if valid(i + 1):
                    h1_split(i + 1)
                if valid(i - 1):
                    hidden(i - 1, 1)
                if valid(i):
                    out_norm(i)
                if valid(i - 1):
                    hidden(i - 1, 2)

            phase_a(dve, iteration)

            for g in range(NG):
                dve.wait_ge(sgt_ps, g + 1)
                dve.tensor_copy(ROW[0][:, :].rearrange("r (p t) -> r t p", t=T),
                                PC[:, 0:S].rearrange("r (t p) -> r t p", t=T)).then_inc(row_ready, 1)
                dve.wait_ge(row_ready, g + 1)
                if g >= 1:
                    dve.wait_ge(tops_t_ps, g)
                steps = g * (3 * (CAP // 8) + 1)
                for r in range(CAP // 8):
                    src, dst = ROW[r % 2], ROW[1 - r % 2]
                    best = TOPV[:, 0, 8 * r:8 * r + 8]
                    dve.max(best, src[:, :]).then_inc(top_step, 1)
                    dve.wait_ge(top_step, steps + 3 * r + 1)
                    dve.max_index(TOPU[:, 8 * r:8 * r + 8], best, src[:, :]).then_inc(top_step, 1)
                    dve.match_replace(dst[:, :], best, src[:, :], -1.0).then_inc(top_step, 1)
                    dve.wait_ge(top_step, steps + 3 * r + 3)
                for h in range(2):
                    last = dve.tensor_scalar(TOPI[:, h, :], TOPU[:, :], const(C_BASE), float(g * GROUP * S), ALU.add,
                                             ALU.add)
                last.then_inc(top_step, 1)
                dve.tensor_copy(TOPV[:, 1, :], TOPV[:, 0, :]).then_inc(tops_ready, 1)
                dve.wait_ge(tops_t_ps, g + 1)
                for h in range(2):
                    rows = slice(h * CAP, (h + 1) * CAP)
                    for o, dst in ((512, IDX), (512 + P, WGT)):
                        last = dve.tensor_copy(
                            dst[rows, :, g * TT:(g + 1) * TT],
                            PC[rows, o:o + P].rearrange("p (q h e) -> p h e q", h=2, e=E)[:, h])
                last.then_inc(tops_read, 1)
            dve.wait_ge(tops_read, NG)
            dve.engine_nop().then_inc(slots_ready, 1)
            dve.wait_ge(pairs_in, 32)

            def rows_lo(s, p):
                dve.wait_ge(tx_hi, s + 1)
                split_lo(XT[p][:, LO, :, :].rearrange("p k s -> p (k s)"), PC[:, 1024:],
                         XT[p][:, HI, :, :].rearrange("p k s -> p (k s)")).then_inc(tx_lo, 1)

            def weigh(e, g, tiles):
                s = e * NG + g
                for t in tiles:
                    dve.wait_ge(edown_done, s * TT + (t // 2 + 1) * 2)
                    if t == 0:
                        wait(dve, scattered[(g - 2) % NG], (e + (1 if g >= 2 else 0)) * (TT * 16))
                    dve.scalar_tensor_tensor(X1[:, g % 2, t * D:(t + 1) * D], PD[:, t * D:(t + 1) * D],
                                             WCUR[g][:, t:t + 1], PAIRS[:, g * TT + t, :], ALU.mult,
                                             ALU.mult).then_inc(eo_ready, 1)

            def step(e, p, g, first=False, last=False):
                s = e * NG + g
                if first:
                    rows_lo(0, 0)
                if g >= 1 and not (isinstance(e, int) and e == E - 1):
                    dve.wait_ge(w_hi, e * 3 + 4 + g)
                    cols = slice((g - 1) * WCOLS, g * WCOLS)
                    split_lo(W[p][:, LO, cols], STAGE[:, cols], W[p][:, HI, cols]).then_inc(w_lo, 1)
                for fc in range(KF):
                    bank = PG if fc % 2 == 0 else PC[:, 0:1024]
                    dve.wait_ge(egelu_done, s * KF + fc + 1)
                    wait(dve, ehid_hi, s * KF + fc - 1)
                    wait(dve, ehid_lo, s * KF + fc - 1)
                    dve.tensor_tensor(HM[:, fc % 2, :], GEL[:, fc % 2, :], bank[:, S:], ALU.mult).then_inc(emul_done, 1)
                    if fc == 2 and not last:
                        rows_lo(s + 1, (g + 1) % 2)
                    dve.wait_ge(ehid_hi, s * KF + fc + 1)
                    dve.tensor_tensor(H[g % 2][:, LO, fc, :], HM[:, fc % 2, :], H[g % 2][:, HI, fc, :].bitcast(F32),
                                      ALU.subtract).then_inc(ehid_lo, 1)
                    if fc in (0, 1) and not first:
                        weigh(e if g else e - 1, (g - 1) % NG, (2 * fc, 2 * fc + 1))
                if last:
                    weigh(e, g, range(TT))

            phase_b(dve, step)

        @block.gpsimd
        def _(pool):
            pool.wait_ge(consts_in, 16)
            pool.wait_ge(rot_sq, 1)
            pool.tensor_tensor(RN[:, :, :].rearrange("p a k -> p (a k)"), RN[:, :, :].rearrange("p a k -> p (a k)"),
                               const(C_HALF, 3 * KD), ALU.pow).then_inc(rot_rn, 1)

            def rstd(j, mv, ve, rs, n):
                wait_apart(pool, mv, n + 1)
                pool.tensor_scalar(RS[j][:, :], MV[j][:, :, 1], EPS, None, ALU.add).then_inc(ve, 1)
                pool.wait_ge(ve, n + 1)
                pool.tensor_tensor(RS[j][:, :], RS[j][:, :], const(C_HALF, T), ALU.pow).then_inc(rs, 1)

            def hidden_lo(n, fc):
                pool.wait_ge(hid_hi, n * KF + fc + 1)
                pool.tensor_tensor(HID[:, LO, fc, :], HM[:, fc % 2, :], HID[:, HI, fc, :].bitcast(F32),
                                   ALU.subtract).then_inc(hid_lo, 1)

            def iteration(i, p, half):
                if valid(i - 1):
                    pool.wait_ge(u_read, i)
                    pool.tensor_tensor(X1[:, 1 - p, :], TMP[:, :, :].rearrange("p t d -> p (t d)"), X[:, 1 - p, :],
                                       ALU.add).then_inc(x1_ready, 1)
                    rstd(1, mv2, ve2, rs2, i - 1)
                if valid(i - 2):
                    hidden_lo(i - 2, 3)
                if valid(i + 1):
                    rstd(0, mv1, ve1, rs1, i + 1)
                if valid(i - 2):
                    pool.wait_ge(y_read, i - 1)
                    pool.tensor_tensor(Y[:, :, :].rearrange("p t d -> p (t d)"),
                                       Y[:, :, :].rearrange("p t d -> p (t d)"), X1[:, p, :],
                                       ALU.add).then_inc(y_ready, 1)
                if valid(i - 1):
                    hidden_lo(i - 1, 0)
                    hidden_lo(i - 1, 1)
                if valid(i):
                    pool.wait_ge(norm_sq, i + 1)
                    pool.tensor_tensor(FAC[:, :], NSQ[:, :], const(C_HALF, T), ALU.pow).then_inc(fac_ready, 1)
                if valid(i - 1):
                    hidden_lo(i - 1, 2)

            phase_a(pool, iteration)

            pool.wait_ge(y_stored, 16 * B)
            pool.wait_ge(h2_stored, 16 * B)
            pool.wait_ge(slots_ready, 1)

            def gather(e, g, s):
                j = g % NG
                wait(pool, tx_done, s - 1)
                wait(pool, scattered[j], e * (TT * 16))
                pool.tensor_copy(ICUR[j][:, :], IDX[:, bass.ds(e, 1), g * TT:(g + 1) * TT].rearrange("p o q -> p (o q)"))
                pool.tensor_copy(WCUR[j][:, :], WGT[:, bass.ds(e, 1), g * TT:(g + 1) * TT].rearrange(
                    "p o q -> p (o q)")).then_inc(cur_ready, 1)
                wait_apart(pool, cur_ready, s + 1)
                for t in range(TT):
                    pool.indirect_dma_start(
                        out=X[:, g % 2, t * D:(t + 1) * D], out_offset=None, in_=h2_dram,
                        in_offset=bass.IndirectOffsetOnAxis(ap=ICUR[j][:, t:t + 1], axis=0)).then_inc(gathered[g % 2], 16)

            def scatter(e, g, s):
                wait_apart(pool, eo_ready, (s + 1) * TT)
                for t in range(TT):
                    pool.indirect_dma_start(
                        out=out_rows, out_offset=bass.IndirectOffsetOnAxis(ap=ICUR[g][:, t:t + 1], axis=0),
                        in_=X1[:, g % 2, t * D:(t + 1) * D], in_offset=None,
                        compute_op=ALU.add).then_inc(scattered[g], 16)

            def step(e, p, g, first=False, last=False):
                s = e * NG + g
                if first:
                    gather(0, 0, 0)
                if not last:
                    en, gn = (e, g + 1) if g + 1 < NG else (e + 1, 0)
                    gather(en, gn, s + 1)
                if not first:
                    ep, gp = (e, g - 1) if g else (e - 1, NG - 1)
                    scatter(ep, gp, s - 1)
                if last:
                    scatter(e, g, s)

            phase_b(pool, step)
            for g in range(NG):
                pool.wait_ge(scattered[g], E * TT * 16)


def kernel(**inputs):
    import numpy as np
    import concourse.bacc as bacc
    from concourse.bass_utils import run_bass_kernel_spmd

    a = {k: np.asarray(v) for k, v in inputs.items()}

    def in_features(w):
        w = np.swapaxes(w, -1, -2)
        lead, (i, o) = w.shape[:-2], w.shape[-2:]
        w = w.reshape(*lead, i // P, P, o)
        return np.ascontiguousarray(np.swapaxes(w, -2, -3).reshape(*lead, P, i // P * o))

    consts = np.zeros((P, C_ALL), np.float32)
    rows = np.arange(P)
    consts[:, C_ID:C_ID + P] = np.eye(P)
    consts[rows, C_SWAP + (rows ^ 1)] = 1
    consts[:, C_EVEN] = rows % 2 == 0
    consts[:, C_ODD] = rows % 2 == 1
    consts[:, C_SIGN] = 1 - 2 * (rows % 2)
    consts[:, C_BASE] = rows // E * S
    consts[:, C_HALF:] = -0.5

    arrays = {
        "x": a["L0_attn_Q"],
        "rot": np.ascontiguousarray(a["L0_attn_rot_w"].reshape(3, KD, P).transpose(2, 0, 1).reshape(P, 3 * KD)),
        "scale": a["L0_attn_scale"].reshape(1, 1),
        "bias": a["L0_attn_bias"].reshape(1, 1),
        "gate_t": in_features(a["L0_ffn_gate_w"]),
        "wg": in_features(a["L0_ffn_Wg"]),
        "wu": in_features(a["L0_ffn_Wu"]),
        "wd": in_features(a["L0_ffn_Wd"]),
        "wsg": in_features(a["L0_ffn_Ws_g"]),
        "wsu": in_features(a["L0_ffn_Ws_u"]),
        "wsd": in_features(a["L0_ffn_Ws_d"]),
        "c": a["L0_c"],
        "wmod": a["L0_wmod"],
        "consts": consts,
    }
    nc = bacc.Bacc("TRN2", target_bir_lowering=False, num_devices=1)
    arrays = {k: np.ascontiguousarray(v) for k, v in arrays.items()}
    dram = {k: nc.dram_tensor(f"in_{k}", v.shape, mybir.dt.from_np(v.dtype), kind="ExternalInput").ap()
            for k, v in arrays.items()}
    out = nc.dram_tensor("out_0", (B, S, D), F32, kind="ExternalOutput").ap()
    block_kernel(nc, dram["x"], dram["rot"], dram["scale"], dram["bias"], dram["gate_t"],
                 (dram["wg"], dram["wu"], dram["wd"]), (dram["wsg"], dram["wsu"], dram["wsd"]),
                 dram["c"], dram["wmod"], dram["consts"], out)
    r = run_bass_kernel_spmd(nc, [{f"in_{k}": v for k, v in arrays.items()}], core_ids=[0])
    return r.results[0]["out_0"]
```

```python
from contextlib import ExitStack

import concourse.bass as bass
from concourse import mybir

ALU = mybir.AluOpType
ACT = mybir.ActivationFunctionType
AX = mybir.AxisListType
F32 = mybir.dt.float32
F32R = mybir.dt.float32r
U32 = mybir.dt.uint32

P = 128
B, S, D = 32, 512, 256
E, F = 16, 512
CAP = S * 2 // E
T = S // P
KD = D // P
KF = F // P
GROUP = P // E
NG = B // GROUP
TT = GROUP * CAP // P
WCOLS = KD * F
NMOD = 4
GA, SB, CB, GB = range(NMOD)
EPS = 1e-5
HI, LO = 0, 1
C_ID, C_SWAP = 0, P
C_EVEN, C_ODD, C_SIGN, C_BASE = range(2 * P, 2 * P + 4)
C_HALF = C_BASE + NG
C_ALL = C_HALF + max(T, 3 * KD)


def block_kernel(nc, x, rot, scale, bias, gate_t, w_exp, w_sh, c, wmod, consts, out):
    h2_dram = nc.dram_tensor("h2_rows", (B * S, D), F32).ap()
    mod_dram = nc.dram_tensor("mod_rows", (B, NMOD * D), F32).ap()
    x_v = x.rearrange("b (p t) d -> b p (t d)", t=T)
    out_v = out.rearrange("b (p t) d -> b p (t d)", t=T)
    out_rows = out.rearrange("b s d -> (b s) d")
    h2_v = h2_dram.rearrange("(b p t) d -> b p (t d)", b=B, t=T)

    with ExitStack() as ctx:
        def sb(name, shape, dt=F32):
            return ctx.enter_context(nc.sbuf_tensor(name, shape, dt))

        def sem(name):
            return ctx.enter_context(nc.semaphore(name))

        W = [sb(f"weights{j}", [P, 2, 3 * WCOLS], F32R) for j in range(2)]
        XT = [sb(f"x_t{j}", [P, 2, KD, S], F32R) for j in range(2)]
        H = [sb(f"hidden{j}", [P, 2, KF, S], F32R) for j in range(2)]
        K_T = sb("k_t", [P, 2, KD, S], F32R)
        V = sb("v", [P, 2, T, D], F32R)
        ROTK = sb("rot_k", [P, 2, KD, P], F32R)
        ROTV = sb("rot_v", [P, 2, KD, P], F32R)
        GW = sb("gate_w", [P, 2, KD, E], F32R)
        H1_T, H2_T = XT
        HID = H[0]
        A_T = H[1]

        X = sb("x_rows", [P, 2, T * D])
        X1 = sb("x1_rows", [P, 2, T * D])
        PAIRS = sb("pairs", [P, B // 2, D])
        STAGE = sb("stage", [P, 3 * WCOLS])
        TMP = sb("tmp_rows", [P, T, D])
        Y = sb("y_rows", [P, T, D])
        GEL = sb("gelu", [P, 2, S])
        HM = sb("hidden_f32", [P, 2, S])
        SG = sb("scores", [P, T, B, E])
        SQ = sb("squares", [P, D])
        ROW = [sb(f"score_rows{j}", [P, S]) for j in range(2)]
        CONST = sb("consts", [P, C_ALL])
        pairs_flat = PAIRS[:, :, :].rearrange("p a d -> p (a d)")
        EXPS = pairs_flat[:, 0:T * S].rearrange("p (t s) -> p t s", t=T)
        MODB = pairs_flat[:, T * S:].rearrange("p (j m d) -> p j m d", j=2, m=NMOD)
        WMOD = pairs_flat[:, 0:KD * 6 * D].rearrange("p (k n) -> p k n", k=KD)
        XN = STAGE[:, 0:T * D].rearrange("p (t d) -> p t d", t=T)
        H2 = STAGE[:, T * D:2 * T * D].rearrange("p (t d) -> p t d", t=T)
        H1_F = STAGE[:, 2 * T * D:].rearrange("p (k s) -> p k s", k=KD)
        mods = SG[:, :, :, :].rearrange("p t b e -> p (t b e)")[0:B, 0:NMOD * D]
        W_RAW = (X1[:, 0, :], X1[:, 1, :], Y[:, :, :].rearrange("p t d -> p (t d)"))

        ROT = sb("rot_raw", [P, 3, KD])
        ROT_SW = sb("rot_swapped", [P, 3, KD])
        COS = sb("cosines", [P, 3, KD])
        SIN = sb("sines", [P, 3, KD])
        RN = sb("rot_norm", [P, 3, KD])
        CS = sb("k_cos_sin", [P, 4, KD])
        ROTF = sb("rot_f32", [P, 2, KD, P])
        SCB = sb("scale_bias", [P, 8])
        GWF = sb("gate_f32", [P, KD, E])
        CIN = sb("cond", [B, D])
        CACT = sb("cond_silu", [B, D])
        CACT_T = sb("cond_t", [P, KD, B])
        SGNS = sb("mod_signs", [B, 3, D])
        SACA = sb("sa_ca_t", [P, 2, KD, B])
        ST = [sb(f"bn_stats{j}", [P, T, 6]) for j in range(2)]
        MV = [sb(f"mean_var{j}", [P, T, 2]) for j in range(2)]
        RS = [sb(f"rstd{j}", [P, T]) for j in range(2)]
        NM = sb("neg_max", [P, T])
        NB = sb("exp_bias", [P, T])
        Z = sb("exp_sum", [P, T])
        ZZ = sb("exp_sum_sq", [P, T])
        SSQ = sb("sum_squares", [P, T])
        NSQ = sb("norm_squares", [P, T])
        FAC = sb("out_factor", [P, T])
        GMX = sb("gate_max", [P, T])
        GLT = sb("gate_logits_t", [E, S])
        GL = sb("gate_logits", [P, T, E])
        GEX = sb("gate_exp", [P, T, E])
        GS = sb("gate_sum", [P, T])
        GR = sb("gate_rsum", [P, T])
        TOPV = sb("top_values", [P, 2, CAP])
        BESTV = sb("best_values", [P, 8])
        BESTU = sb("best_positions", [P, 8], U32)
        TOPI = sb("top_indices", [P, 2, CAP])
        IDX = sb("slot_token", [P, E, NG * TT], U32)
        WGT = sb("slot_weight", [P, E, NG * TT])
        ICUR = [sb(f"step_token{j}", [P, TT], U32) for j in range(4)]
        WCUR = [sb(f"step_weight{j}", [P, TT]) for j in range(4)]

        PS = ctx.enter_context(nc.psum_tensor("ps", [P, 4096], F32))
        PC, PD, PG = PS[:, 0:2048], PS[:, 2048:3072], PS[:, 3072:4096]

        IDENT = CONST[:, C_ID:C_ID + P]
        SWAP = CONST[:, C_SWAP:C_SWAP + P]

        def const(j, n=1):
            return CONST[:, j:j + n]

        consts_in, rot_in, cond_in, wmod_in, gate_in, scal_in = map(
            sem, ("consts_in", "rot_in", "cond_in", "wmod_in", "gate_in", "scal_in"))
        w_in, w0_in, wmod2_in = sem("w_in"), sem("w0_in"), sem("wmod2_in")
        saca_ps, saca_ready, mods_raw = map(sem, ("saca_ps", "saca_ready", "mods_raw"))
        dve_setup, rot_sw_ps, rot_sq, rot_rn, silu_done, cond_t_ps, cond_t, mods_ps = map(
            sem, ("dve_setup", "rot_sw_ps", "rot_sq", "rot_rn", "silu_done", "cond_t_ps", "cond_t", "mods_ps"))
        mods_ready, rot_ready, gw_ready, mods_stored = map(
            sem, ("mods_ready", "rot_ready", "gw_ready", "mods_stored"))
        w_hi, w_lo = sem("w_hi"), sem("w_lo")
        x_in = [sem("x_in0"), sem("x_in1")]
        mod_in = [sem("mod_in0"), sem("mod_in1")]
        st1, mv1, ve1, rs1, xn_ready = map(sem, ("st1", "mv1", "ve1", "rs1", "xn_ready"))
        xt_done, h1f_ready, h1_hi, h1_lo = map(sem, ("xt_done", "h1f_ready", "h1_hi", "h1_lo"))
        k_done, k_hi, k_lo, v_done, v_hi, v_lo = map(sem, ("k_done", "k_hi", "k_lo", "v_done", "v_hi", "v_lo"))
        s_done, nmax, ebias, exp_done = map(sem, ("s_done", "nmax", "ebias", "exp_done"))
        at_done, at_hi, at_lo, av_done = map(sem, ("at_done", "at_hi", "at_lo", "av_done"))
        ssq_done, zz_ready, norm_sq, fac_ready, u_read, x1_ready = map(
            sem, ("ssq_done", "zz_ready", "norm_sq", "fac_ready", "u_read", "x1_ready"))
        st2, mv2, ve2, rs2, cent2, h2_ready, h2_stored = map(
            sem, ("st2", "mv2", "ve2", "rs2", "cent2", "h2_ready", "h2_stored"))
        h2t_done, h2t_hi, h2t_lo = map(sem, ("h2t_done", "h2t_hi", "h2t_lo"))
        gate_done, gate_read, gate_t_done, gmax_ready, gl_ready, gexp_done, gsum, grs, sg_ready = map(
            sem, ("gate_done", "gate_read", "gate_t_done", "gmax_ready", "gl_ready", "gexp_done", "gsum", "grs", "sg_ready"))
        gu_done, gelu_done, mul_done, hid_hi, hid_lo = map(
            sem, ("gu_done", "gelu_done", "mul_done", "hid_hi", "hid_lo"))
        down_done, y_read, y_ready, y_stored = map(sem, ("down_done", "y_read", "y_ready", "y_stored"))
        pairs_in, group_set, sgt_ps, row_ready, top_step, top_kept, tops_t_ps, tops_read = map(
            sem, ("pairs_in", "group_set", "sgt_ps", "row_ready", "top_step", "top_kept", "tops_t_ps", "tops_read"))
        cur_ready = sem("cur_ready")
        gathered = [sem(f"gathered{j}") for j in range(2)]
        tx_done, tx_hi, tx_lo = map(sem, ("tx_done", "tx_hi", "tx_lo"))
        egu_done, egelu_done, emul_done, ehid_hi, ehid_lo, edown_done, eo_ready = map(
            sem, ("egu_done", "egelu_done", "emul_done", "ehid_hi", "ehid_lo", "edown_done", "eo_ready"))
        scattered = [sem(f"scattered{j}") for j in range(NG)]

        def valid(n):
            return not isinstance(n, int) or 0 <= n < B

        def wait(e, s, count):
            if not isinstance(count, int) or count > 0:
                e.wait_ge(s, count)

        def wait_apart(e, s, count):
            if not isinstance(count, int):
                e.compute_val(count)
            e.wait_ge(consts_in, 16)
            wait(e, s, count)

        def at(i, n):
            return isinstance(i, int) and i == n

        def flat(a):
            return a.rearrange("p a b -> p (a b)")

        def phase_a(e, iteration):
            for i in (-1, 0, 1, 2):
                iteration(i, i % 2, i // 2)
            with e.Fori(1, (B - 2) // 2) as half:
                iteration(half * 2 + 1, 1, half)
                iteration(half * 2 + 2, 0, half + 1)
            for i in (B - 1, B, B + 1):
                iteration(i, i % 2, i // 2)

        def phase_a_with_tops(e, iteration):
            for i in (-1, 0, 1, 2):
                iteration(i, i % 2, i // 2)
            with e.Fori(1, 4) as half:
                iteration(half * 2 + 1, 1, half)
                iteration(half * 2 + 2, 0, half + 1)
            iteration(9, 1, 4)
            iteration(10, 0, 5, start=0)
            with e.Fori(0, 2) as g:
                with e.Fori(0, GROUP // 2 - 1) as q:
                    i = g * 8 + q * 2 + 11
                    iteration(i, 1, g * 4 + q + 5, ((g, q * 2, g * 8 + q * 2),))
                    iteration(i + 1, 0, g * 4 + q + 6, ((g, q * 2 + 1, g * 8 + q * 2 + 1),))
                iteration(g * 8 + 17, 1, g * 4 + 8, ((g, 6, g * 8 + 6),))
                iteration(g * 8 + 18, 0, g * 4 + 9, ((g, 7, g * 8 + 7),), finish=g, start=g + 1)
            for i in range(27, B + 2):
                r = 2 * (i - 27)
                rounds = ((2, r, 16 + r), (2, r + 1, 17 + r)) if r < 8 else ()
                iteration(i, i % 2, i // 2, rounds, finish=2 if i == B - 1 else None)

        def phase_b(e, step):
            for g in range(NG):
                step(0, 0, g, first=g == 0)
            with e.Fori(0, (E - 2) // 2) as ii:
                for j in (1, 2):
                    for g in range(NG):
                        step(ii * 2 + j, j % 2, g)
            for g in range(NG):
                step(E - 1, (E - 1) % 2, g, last=g == NG - 1)

        def wg(j, part, k, fc):
            return W[j][:, part, k * F + fc * P:k * F + fc * P + P]

        def wu(j, part, k, fc):
            return W[j][:, part, WCOLS + k * F + fc * P:WCOLS + k * F + fc * P + P]

        def wd(j, part, fc):
            return W[j][:, part, 2 * WCOLS + fc * D:2 * WCOLS + fc * D + D]

        def other_bank(n, fc):
            return at(n, B - 1) and fc % 2 == 1 or at(n, B - 2) and fc == KF - 1

        def gu_bank(n, fc):
            return PC[:, 0:2 * S] if other_bank(n, fc) else PG

        block = ctx.enter_context(nc.Block())

        @block.sync
        def _(sp):
            sp.dma_start(CONST[:, :], consts).then_inc(consts_in, 16)
            sp.dma_start(CIN[:, :], c).then_inc(cond_in, 16)
            sp.dma_start(ROT[:, :, :].rearrange("p a k -> p (a k)"), rot).then_inc(rot_in, 16)
            sp.dma_start(X[:, 0, :], x_v[0]).then_inc(x_in[0], 16)
            sp.dma_start(SCB[:, 0:1], scale.to_broadcast((P, 1))).then_inc(scal_in, 16)
            sp.dma_start(SCB[:, 1:2], bias.to_broadcast((P, 1))).then_inc(scal_in, 16)
            wmod_v = wmod.rearrange("(k p) n -> p k n", p=P)
            sp.dma_start(WMOD[:, :, 0:2 * D], wmod_v[:, :, 0:2 * D]).then_inc(wmod_in, 16)
            sp.dma_start(WMOD[:, :, 2 * D:], wmod_v[:, :, 2 * D:]).then_inc(wmod2_in, 16)
            sp.dma_start(GWF[:, :, :].rearrange("p k e -> p (k e)"), gate_t).then_inc(gate_in, 16)
            for m in range(3):
                sp.dma_start(W_RAW[m], w_sh[m]).then_inc(w_in, 16)

            def iteration(i, p, half):
                if at(i, B - 1):
                    sp.wait_ge(xt_done, B)
                    sp.wait_ge(h1_lo, B)
                    for m in (0, 2):
                        sp.dma_start(STAGE[:, m * WCOLS:(m + 1) * WCOLS], w_exp[m][0]).then_inc(w0_in, 16)
                if valid(i + 1) and not (isinstance(i, int) and i < 0):
                    wait(sp, x1_ready, i)
                    sp.dma_start(X[:, 1 - p, :], x_v[i + 1]).then_inc(x_in[1 - p], 16)
                if valid(i - 1):
                    wait(sp, h2_ready, i)
                    sp.dma_start(h2_v[i - 1], H2.rearrange("p t d -> p (t d)")).then_inc(h2_stored, 16)
                if at(i, B):
                    sp.wait_ge(h2t_done, KD * B)
                    sp.wait_ge(h2_stored, 16 * B)
                    sp.dma_start(STAGE[:, WCOLS:2 * WCOLS], w_exp[1][0]).then_inc(w_in, 16)
                if valid(i - 2):
                    wait(sp, y_ready, i - 1)
                    sp.dma_start(out_v[i - 2], Y[:, :, :].rearrange("p t d -> p (t d)")).then_inc(y_stored, 16)
                if at(i, 0):
                    sp.wait_ge(mods_ready, 1)
                    sp.dma_start(mod_dram, mods).then_inc(mods_stored, 16)
                    sp.wait_ge(mods_stored, 16)
                if valid(i):
                    wait(sp, y_read, i - 1)
                    sp.dma_start(MODB[:, p, :, :].rearrange("p m d -> p (m d)"),
                                 mod_dram[bass.ds(i, 1), :].to_broadcast((P, NMOD * D))).then_inc(mod_in[p], 16)

            phase_a(sp, iteration)

            sp.wait_ge(exp_done, T * B)
            sp.wait_ge(at_done, T * B)
            sp.wait_ge(y_read, B)
            for half in range(2):
                gb = mod_dram.rearrange("(a h) (m d) -> h m a d", h=2, m=NMOD)[half, GB]
                sp.dma_start(PAIRS[half * CAP:(half + 1) * CAP, :, :],
                             gb.unsqueeze(0).to_broadcast((CAP, B // 2, D))).then_inc(pairs_in, 16)

            def step(e, p, g, first=False, last=False):
                if g == 0 and not (isinstance(e, int) and e == E - 1):
                    sp.wait_ge(w_hi, e * 3 + 6)
                    sp.wait_ge(w_lo, e * 3 + 6)
                    for m in range(3):
                        sp.dma_start(STAGE[:, m * WCOLS:(m + 1) * WCOLS], w_exp[m][e + 1]).then_inc(w_in, 16)

            phase_b(sp, step)
            sp.wait_ge(y_stored, 16 * B)

        @block.tensor
        def _(pe):
            def mm3(o, lhs, rhs, start, stop):
                pe.matmul(o, lhs(HI), rhs(HI), start=start, stop=False)
                pe.matmul(o, lhs(HI), rhs(LO), start=False, stop=False)
                return pe.matmul(o, lhs(LO), rhs(HI), start=False, stop=stop)

            pe.wait_ge(consts_in, 16)
            pe.wait_ge(rot_in, 16)
            pe.matmul(PG[:, 0:3 * KD], SWAP, ROT[:, :, :].rearrange("p a k -> p (a k)"),
                      start=True, stop=True).then_inc(rot_sw_ps, 1)
            pe.wait_ge(silu_done, 1)
            for k in range(KD):
                mm = pe.transpose(PG[:, 512 + k * B:512 + (k + 1) * B], CACT[:, k * P:(k + 1) * P], IDENT[0:B, 0:B])
            mm.then_inc(cond_t_ps, 1)
            pe.wait_ge(cond_t, 1)
            pe.wait_ge(wmod_in, 16)
            for j in range(2):
                for m in range(KD):
                    n = j * KD + m
                    for k in range(KD):
                        mm = pe.matmul(PG[:, n * B:(n + 1) * B], WMOD[:, k, j * D + m * P:j * D + (m + 1) * P],
                                       CACT_T[:, k, :], start=k == 0, stop=k == KD - 1)
            mm.then_inc(saca_ps, 1)
            def modulations():
                pe.wait_ge(wmod2_in, 16)
                for n in range(2):
                    for k in range(KD):
                        mm = pe.matmul(PD[0:B, n * 512:(n + 1) * 512], CACT_T[:, k, :],
                                       WMOD[:, k, 2 * D + n * 512:2 * D + (n + 1) * 512], start=k == 0, stop=k == KD - 1)
                mm.then_inc(mods_ps, 1)

            def x_transposes(n):
                wait(pe, xn_ready, n + 1)
                wait(pe, at_hi, n * T)
                wait(pe, at_lo, n * T)
                for k in range(KD):
                    for t in range(T):
                        mm = pe.transpose(PC[:, k * S + t * P:k * S + (t + 1) * P], XN[:, t, k * P:(k + 1) * P], IDENT)
                mm.then_inc(xt_done, 1)

            def k_and_v(n):
                if at(n, 0):
                    pe.wait_ge(rot_ready, 1)
                wait(pe, h1_hi, n + 1)
                wait(pe, h1_lo, n + 1)
                for k in range(KD):
                    mm = mm3(PC[:, (KD + k) * S:(KD + k + 1) * S], lambda a: ROTK[:, a, k, :],
                             lambda a: H1_T[:, a, k, :], True, True)
                mm.then_inc(k_done, 1)
                for t in range(T):
                    for k in range(KD):
                        mm = mm3(PC[:, t * D + k * P:t * D + (k + 1) * P],
                                 lambda a: H1_T[:, a, k, t * P:(t + 1) * P], lambda a: ROTV[:, a, k, :], True, True)
                mm.then_inc(v_done, 1)

            def scores(n):
                wait(pe, k_hi, n + 1)
                wait(pe, k_lo, n + 1)
                wait(pe, v_hi, n + 1)
                wait(pe, v_lo, n + 1)
                for t in range(T):
                    for k in range(KD):
                        mm = mm3(PC[:, t * S:(t + 1) * S], lambda a: H1_T[:, a, k, t * P:(t + 1) * P],
                                 lambda a: K_T[:, a, k, :], k == 0, k == KD - 1)
                    mm.then_inc(s_done, 1)

            def a_transposes(n):
                for t in range(T):
                    wait(pe, exp_done, n * T + t + 1)
                    for q in range(T):
                        mm = pe.transpose(PC[:, t * S + q * P:t * S + (q + 1) * P], EXPS[:, t, q * P:(q + 1) * P],
                                          IDENT)
                    mm.then_inc(at_done, 1)

            def a_times_v(n, half):
                if at(n, 0):
                    pe.wait_ge(mods_raw, 1)
                for t in (2 * half, 2 * half + 1):
                    wait(pe, at_hi, n * T + t + 1)
                    wait(pe, at_lo, n * T + t + 1)
                    if t == 2:
                        wait(pe, gl_ready, n)
                    for q in range(T):
                        mm = mm3(PD[:, t * D:(t + 1) * D], lambda a: A_T[:, a, t, q * P:(q + 1) * P],
                                 lambda a: V[:, a, q, :], q == 0, q == T - 1)
                    mm.then_inc(av_done, 1)

            def h2_transposes(n):
                wait(pe, h2_ready, n + 1)
                wait(pe, mul_done, n * KF)
                for k in range(KD):
                    for t in range(T):
                        mm = pe.transpose(PG[:, k * S + t * P:k * S + (t + 1) * P], H2[:, t, k * P:(k + 1) * P], IDENT)
                    mm.then_inc(h2t_done, 1)

            def gate(n):
                if at(n, 0):
                    pe.wait_ge(gw_ready, 1)
                wait(pe, y_read, n)
                for k in range(KD):
                    wait(pe, h2t_hi, n * KD + k + 1)
                    wait(pe, h2t_lo, n * KD + k + 1)
                    mm = mm3(PD[0:E, 512:512 + S], lambda a: GW[:, a, k, :], lambda a: H2_T[:, a, k, :],
                             k == 0, k == KD - 1)
                mm.then_inc(gate_done, 1)

            def gate_transposes(n):
                wait_apart(pe, gate_read, n + 1)
                for t in range(T):
                    mm = pe.transpose(PD[:, 512 + t * E:512 + (t + 1) * E], GLT[:, t * P:(t + 1) * P],
                                      IDENT[0:E, 0:E])
                mm.then_inc(gate_t_done, 1)

            def gate_up(n, fc):
                if at(n, 0):
                    pe.wait_ge(w_hi, 3)
                    pe.wait_ge(w_lo, 3)
                wait(pe, h2t_hi, (n + 1) * KD)
                wait(pe, h2t_lo, (n + 1) * KD)
                alternates = other_bank(n, fc) or at(n, B - 1) and fc > 0
                wait(pe, mul_done, n * KF + fc - (1 if alternates else 0))
                for half, w in ((0, wg), (1, wu)):
                    for k in range(KD):
                        mm = mm3(gu_bank(n, fc)[:, half * S:(half + 1) * S], lambda a: w(0, a, k, fc),
                                 lambda a: H2_T[:, a, k, :], k == 0, k == KD - 1)
                mm.then_inc(gu_done, 1)

            def down(n):
                wait(pe, u_read, min(n + 2, B) if isinstance(n, int) else n + 2)
                if isinstance(n, int) and n == B - 1:
                    wait(pe, gl_ready, B)
                for t in range(T):
                    for fc in range(KF):
                        if t == 0:
                            wait(pe, hid_hi, n * KF + fc + 1)
                            wait(pe, hid_lo, n * KF + fc + 1)
                        mm = mm3(PD[:, t * D:(t + 1) * D], lambda a: HID[:, a, fc, t * P:(t + 1) * P],
                                 lambda a: wd(0, a, fc), fc == 0, fc == KF - 1)
                    if t % 2:
                        mm.then_inc(down_done, 1)

            def rows_transposes(e, g):
                s, p = e * NG + g, g % 2
                pe.wait_ge(gathered[p], (e * (NG // 2) + g // 2 + 1) * (TT * 16))
                wait(pe, tx_hi, s * KD)
                wait(pe, tx_lo, s * KD)
                for k in range(KD):
                    for t in range(TT):
                        mm = pe.transpose(PC[:, 1024 + k * S + t * P:1024 + k * S + (t + 1) * P],
                                          X[:, p, t * D + k * P:t * D + (k + 1) * P], IDENT)
                    mm.then_inc(tx_done, 1)

            def score_transposes(g):
                pe.wait_ge(group_set, g + 1)
                for t in range(T):
                    mm = pe.transpose(PC[:, 2 * S + t * P:2 * S + (t + 1) * P], ROW[1][:, t * P:(t + 1) * P], IDENT)
                mm.then_inc(sgt_ps, 1)

            def top_transposes(g):
                pe.wait_ge(top_kept, (g + 1) * (CAP // 8))
                pe.transpose(PC[:, 3 * S:3 * S + P], flat(TOPI[:, :, :]), IDENT)
                pe.transpose(PC[:, 3 * S + P:3 * S + 2 * P], flat(TOPV[:, :, :]), IDENT).then_inc(tops_t_ps, 1)

            def iteration(i, p, half, rounds=(), finish=None, start=None):
                if valid(i):
                    k_and_v(i)
                if valid(i - 2):
                    gate_up(i - 2, 3)
                if valid(i):
                    scores(i)
                if at(i, B + 1):
                    rows_transposes(0, 0)
                if valid(i - 2):
                    down(i - 2)
                if valid(i - 1):
                    h2_transposes(i - 1)
                if valid(i):
                    a_transposes(i)
                if valid(i - 1):
                    gate(i - 1)
                    gate_up(i - 1, 0)
                    gate_transposes(i - 1)
                if valid(i):
                    a_times_v(i, 0)
                if valid(i + 1):
                    x_transposes(i + 1)
                if at(i, -1):
                    modulations()
                if valid(i - 1):
                    gate_up(i - 1, 1)
                if valid(i):
                    a_times_v(i, 1)
                if finish is not None:
                    top_transposes(finish)
                if start is not None:
                    score_transposes(start)
                if valid(i - 1):
                    gate_up(i - 1, 2)
                if finish is not None:
                    wait_apart(pe, tops_read, finish + 1)
                if start is not None:
                    wait_apart(pe, row_ready, start + 1)

            phase_a_with_tops(pe, iteration)
            pe.wait_ge(mul_done, KF * B)

            def e_gate_up(s, g, j, fc):
                if fc == 0:
                    pe.wait_ge(tx_hi, s * KD + KD)
                    pe.wait_ge(tx_lo, s * KD + KD)
                bank = PG if fc % 2 == 0 else PC[:, 0:1024]
                wait(pe, emul_done, s * KF + fc - 1)
                for half, w in ((0, wg), (1, wu)):
                    for k in range(KD):
                        mm = mm3(bank[:, half * S:(half + 1) * S], lambda a: w(j, a, k, fc),
                                 lambda a: XT[g % 2][:, a, k, :], k == 0, k == KD - 1)
                mm.then_inc(egu_done, 1)

            def e_down(s, g, j, tiles):
                for t in tiles:
                    for fc in range(KF):
                        if t == 0:
                            pe.wait_ge(ehid_hi, s * KF + fc + 1)
                            pe.wait_ge(ehid_lo, s * KF + fc + 1)
                        if fc == 0:
                            wait(pe, eo_ready, (s - 1) * TT + (t // 2 + 1) * 2)
                        mm = mm3(PD[:, t * D:(t + 1) * D], lambda a: H[g % 2][:, a, fc, t * P:(t + 1) * P],
                                 lambda a: wd(j, a, fc), fc == 0, fc == KF - 1)
                    mm.then_inc(edown_done, 1)

            def step(e, p, g, first=False, last=False):
                s = e * NG + g
                j = 1 - p
                jd = j if g else 1 - j
                if g == 0:
                    pe.wait_ge(w_hi, e * 3 + 6)
                    pe.wait_ge(w_lo, e * 3 + 6)
                e_gate_up(s, g, j, 0)
                if first:
                    pe.wait_ge(group_set, NG)
                    for t in range(T):
                        mm = pe.transpose(PC[:, t * P:(t + 1) * P], ROW[1][:, t * P:(t + 1) * P], IDENT)
                    mm.then_inc(sgt_ps, 1)
                    pe.wait_ge(row_ready, NG)
                if at(e, 0) and g == 1:
                    pe.wait_ge(y_read, B)
                if not first:
                    e_down(s - 1, g - 1, jd, (0, 1))
                e_gate_up(s, g, j, 1)
                if at(e, 0) and g == 2:
                    pe.wait_ge(eo_ready, TT)
                    pe.wait_ge(top_kept, NG * (CAP // 8))
                    pe.transpose(PD[:, S:S + P], flat(TOPI[:, :, :]), IDENT)
                    pe.transpose(PD[:, S + P:S + 2 * P], flat(TOPV[:, :, :]), IDENT).then_inc(tops_t_ps, 1)
                    pe.wait_ge(tops_read, NG)
                if not first:
                    e_down(s - 1, g - 1, jd, (2, 3))
                e_gate_up(s, g, j, 2)
                if not last:
                    rows_transposes(e, g + 1)
                e_gate_up(s, g, j, 3)
                if last:
                    e_down(s, g, j, range(TT))

            phase_b(pe, step)

        @block.scalar
        def _(act):
            act.wait_ge(cond_in, 16)
            act.activation(CACT[:, :], CIN[:, :], ACT.Silu).then_inc(silu_done, 1)

            def h1_modulate(n):
                if at(n, 0):
                    act.wait_ge(saca_ready, 1)
                act.wait_ge(xt_done, n + 1)
                wait(act, h1_hi, n)
                wait(act, h1_lo, n)
                for k in range(KD):
                    last = act.activation(H1_F[:, k, :], PC[:, k * S:(k + 1) * S], ACT.Identity,
                                          bias=SACA[:, 0, k, bass.ds(n, 1)], scale=SACA[:, 1, k, bass.ds(n, 1)])
                last.then_inc(h1f_ready, 1)

            def hidden(n, fc):
                act.wait_ge(gu_done, n * KF + fc + 1)
                act.activation(GEL[:, fc % 2, :], gu_bank(n, fc)[:, 0:S], ACT.Gelu).then_inc(gelu_done, 1)
                act.wait_ge(mul_done, n * KF + fc + 1)
                wait(act, down_done, n * 2)
                act.copy(HID[:, HI, fc, :], HM[:, fc % 2, :]).then_inc(hid_hi, 1)

            def shared_weights_hi(m):
                act.wait_ge(w_in, 48)
                act.copy(W[0][:, HI, m * WCOLS:(m + 1) * WCOLS], W_RAW[m]).then_inc(w_hi, 1)

            def squares(n, tiles):
                for t in tiles:
                    act.wait_ge(av_done, n * T + (t // 2 + 1) * 2)
                    wait(act, ssq_done, n * T + t)
                    act.activation(SQ[:, :], PD[:, t * D:(t + 1) * D], ACT.Square,
                                   accum_out=SSQ[:, t:t + 1]).then_inc(ssq_done, 1)

            def rows_hi(s, p):
                for k in range(KD):
                    act.wait_ge(tx_done, s * KD + k + 1)
                    act.copy(XT[p][:, HI, k, :], PC[:, 1024 + k * S:1024 + (k + 1) * S]).then_inc(tx_hi, 1)

            def iteration(i, p, half):
                if valid(i):
                    act.wait_ge(k_done, i + 1)
                    act.copy(K_T[:, HI, :, :].rearrange("p k s -> p (k s)"), PC[:, KD * S:]).then_inc(k_hi, 1)
                    act.wait_ge(v_done, i + 1)
                    act.copy(V[:, HI, :, :].rearrange("p t d -> p (t d)"), PC[:, 0:T * D]).then_inc(v_hi, 1)
                if at(i, 0):
                    act.wait_ge(mods_ps, 1)
                    act.copy(mods, PD[0:B, :]).then_inc(mods_raw, 1)
                    for m in range(3):
                        shared_weights_hi(m)
                if valid(i - 2):
                    hidden(i - 2, 3)
                    if at(i, B + 1):
                        act.wait_ge(w_in, 64)
                        act.copy(W[1][:, HI, WCOLS:2 * WCOLS], STAGE[:, WCOLS:2 * WCOLS]).then_inc(w_hi, 1)
                        rows_hi(0, 0)
                    act.wait_ge(gl_ready, i - 1)
                    wait(act, sg_ready, i - 2)
                    act.activation(GEX[:, :, :], GL[:, :, :], ACT.Exp).then_inc(gexp_done, 1)
                if valid(i):
                    for t in range(T):
                        act.wait_ge(ebias, i * T + t + 1)
                        act.activation(EXPS[:, t, :], PC[:, t * S:(t + 1) * S], ACT.Exp, bias=NB[:, t:t + 1],
                                       accum_out=Z[:, t:t + 1]).then_inc(exp_done, 1)
                if valid(i - 1):
                    for k in range(KD):
                        act.wait_ge(h2t_done, (i - 1) * KD + k + 1)
                        act.copy(H2_T[:, HI, k, :], PG[:, k * S:(k + 1) * S]).then_inc(h2t_hi, 1)
                if valid(i):
                    for t in range(T):
                        act.wait_ge(at_done, i * T + t + 1)
                        act.copy(A_T[:, HI, t, :], PC[:, t * S:(t + 1) * S]).then_inc(at_hi, 1)
                if valid(i - 1):
                    act.wait_ge(gate_done, i)
                    wait(act, gate_t_done, i - 1)
                    act.copy(GLT[:, :], PD[0:E, 512:512 + S]).then_inc(gate_read, 1)
                    hidden(i - 1, 0)
                if valid(i):
                    squares(i, (0, 1))
                if valid(i + 1):
                    h1_modulate(i + 1)
                if valid(i - 1):
                    hidden(i - 1, 1)
                if valid(i):
                    squares(i, (2, 3))
                if valid(i - 1):
                    hidden(i - 1, 2)
                if at(i, B):
                    act.wait_ge(w0_in, 32)
                    for m in (0, 2):
                        act.copy(W[1][:, HI, m * WCOLS:(m + 1) * WCOLS],
                                 STAGE[:, m * WCOLS:(m + 1) * WCOLS]).then_inc(w_hi, 1)

            phase_a(act, iteration)
            act.wait_ge(down_done, B * 2)

            def step(e, p, g, first=False, last=False):
                s = e * NG + g
                if g >= 1 and not (isinstance(e, int) and e == E - 1):
                    act.wait_ge(w_in, (e + 1) * 48 + 64)
                    wait(act, edown_done, e * (NG * TT))
                    act.copy(W[p][:, HI, (g - 1) * WCOLS:g * WCOLS],
                             STAGE[:, (g - 1) * WCOLS:g * WCOLS]).then_inc(w_hi, 1)
                for fc in range(KF):
                    bank = PG if fc % 2 == 0 else PC[:, 0:1024]
                    act.wait_ge(egu_done, s * KF + fc + 1)
                    act.activation(GEL[:, fc % 2, :], bank[:, 0:S], ACT.Gelu).then_inc(egelu_done, 1)
                    if fc == 2 and not last:
                        rows_hi(s + 1, (g + 1) % 2)
                    act.wait_ge(emul_done, s * KF + fc + 1)
                    act.copy(H[g % 2][:, HI, fc, :], HM[:, fc % 2, :]).then_inc(ehid_hi, 1)

            phase_b(act, step)

        @block.vector
        def _(dve):
            links = [0]

            def link(ins):
                links[0] += 1
                ins.then_inc(dve_setup, 1)
                dve.wait_ge(dve_setup, links[0])

            def split_lo(o, full, hi):
                return dve.tensor_tensor(o, full, hi.bitcast(F32), ALU.subtract)

            def row_stats(rows, j, st, mv, n):
                for t in range(T):
                    last = dve.bn_stats(ST[j][:, t, :], rows(t))
                last.then_inc(st, 1)
                wait_apart(dve, st, n + 1)
                for t in range(T):
                    last = dve.bn_aggr(MV[j][:, t, :], ST[j][:, t, :])
                last.then_inc(mv, 1)

            def ln1_stats(n, p, loads):
                dve.wait_ge(x_in[p], loads * 16)
                row_stats(lambda t: X[:, p, t * D:(t + 1) * D], 0, st1, mv1, n)

            dve.wait_ge(rot_sw_ps, 1)
            raw, sw = flat(ROT[:, :, :]), flat(ROT_SW[:, :, :])
            cos, sin, rn = (flat(a[:, :, :]) for a in (COS, SIN, RN))
            link(dve.tensor_copy(sw, PG[:, 0:3 * KD]))
            link(dve.tensor_scalar(cos, raw, const(C_EVEN), None, ALU.mult))
            link(dve.scalar_tensor_tensor(cos, sw, const(C_ODD), cos, ALU.mult, ALU.add))
            link(dve.tensor_scalar(sin, raw, const(C_ODD), None, ALU.mult))
            link(dve.scalar_tensor_tensor(sin, sw, const(C_EVEN), sin, ALU.mult, ALU.add))
            link(dve.tensor_tensor(raw, cos, cos, ALU.mult))
            link(dve.tensor_tensor(sw, sin, sin, ALU.mult))
            dve.tensor_tensor(rn, raw, sw, ALU.add).then_inc(rot_sq, 1)
            dve.wait_ge(cond_t_ps, 1)
            dve.tensor_copy(CACT_T[:, :, :].rearrange("p k b -> p (k b)"), PG[:, 512:512 + KD * B]).then_inc(cond_t, 1)
            ln1_stats(0, 0, 1)
            dve.wait_ge(saca_ps, 1)
            dve.tensor_copy(flat(SACA[:, 0, :, :]), PG[:, 0:KD * B])
            dve.tensor_scalar(flat(SACA[:, 1, :, :]), PG[:, KD * B:2 * KD * B], 1.0, None,
                              ALU.add).then_inc(saca_ready, 1)

            def rotations():
                dve.wait_ge(rot_rn, 1)
                link(dve.tensor_tensor(cos, cos, rn, ALU.mult))
                link(dve.tensor_tensor(sin, sin, rn, ALU.mult))
                dve.wait_ge(scal_in, 32)
                r2, cz, ncz = SCB[:, 3:4], SCB[:, 4:5], SCB[:, 5:6]
                link(dve.reciprocal(SCB[:, 2:3], SCB[:, 0:1]))
                link(dve.tensor_scalar(r2, SCB[:, 2:3], 2.0, None, ALU.mult))
                link(dve.tensor_tensor(cz, r2, SCB[:, 1:2], ALU.add))
                link(dve.tensor_scalar(ncz, cz, -1.0, None, ALU.mult))
                link(dve.tensor_tensor(CS[:, 0, :], COS[:, 0, :], COS[:, 1, :], ALU.mult))
                link(dve.tensor_tensor(CS[:, 1, :], SIN[:, 0, :], SIN[:, 1, :], ALU.mult))
                link(dve.tensor_tensor(CS[:, 2, :], COS[:, 0, :], SIN[:, 1, :], ALU.mult))
                link(dve.tensor_tensor(CS[:, 3, :], SIN[:, 0, :], COS[:, 1, :], ALU.mult))
                link(dve.tensor_tensor(CS[:, 0, :], CS[:, 0, :], CS[:, 1, :], ALU.add))
                link(dve.tensor_tensor(CS[:, 2, :], CS[:, 2, :], CS[:, 3, :], ALU.subtract))
                link(dve.tensor_scalar(CS[:, 0, :], CS[:, 0, :], r2, None, ALU.mult))
                link(dve.tensor_scalar(CS[:, 2, :], CS[:, 2, :], r2, const(C_SIGN), ALU.mult, ALU.mult))
                link(dve.tensor_scalar(CS[:, 3, :], SIN[:, 2, :], const(C_SIGN), None, ALU.mult))
                for m, (cc, ss, dst) in enumerate(((CS[:, 0, :], CS[:, 2, :], ROTK), (COS[:, 2, :], CS[:, 3, :], ROTV))):
                    for k in range(KD):
                        link(dve.tensor_scalar(ROTF[:, m, k, :], IDENT, cc[:, k:k + 1], None, ALU.mult))
                        link(dve.scalar_tensor_tensor(ROTF[:, m, k, :], SWAP, ss[:, k:k + 1], ROTF[:, m, k, :],
                                                      ALU.mult, ALU.add))
                    link(dve.tensor_copy(dst[:, HI, :, :], ROTF[:, m, :, :]))
                    link(split_lo(dst[:, LO, :, :], ROTF[:, m, :, :], dst[:, HI, :, :]))
                dve.engine_nop().then_inc(rot_ready, 1)

            def gate_weights():
                dve.wait_ge(gate_in, 16)
                link(dve.tensor_copy(GW[:, HI, :, :], GWF[:, :, :]))
                split_lo(GW[:, LO, :, :], GWF[:, :, :], GW[:, HI, :, :]).then_inc(gw_ready, 1)

            def modulations():
                dve.wait_ge(mods_raw, 1)
                cb = mods[:, CB * D:(CB + 1) * D]
                dve.tensor_scalar(cb, cb, 1.0, None, ALU.add)
                for j in (GA, GB):
                    g = mods[:, j * D:(j + 1) * D]
                    link(dve.tensor_scalar(SGNS[:, 0, :], g, 0.0, 2.0, ALU.is_ge, ALU.mult))
                    link(dve.tensor_scalar(SGNS[:, 0, :], SGNS[:, 0, :], 1.0, None, ALU.subtract))
                    link(dve.tensor_scalar(SGNS[:, 1, :], g, -1.0, None, ALU.mult))
                    link(dve.tensor_tensor(SGNS[:, 2, :], g, SGNS[:, 1, :], ALU.max))
                    link(dve.scalar_tensor_tensor(g, SGNS[:, 2, :], 0.25, SGNS[:, 0, :], ALU.max, ALU.mult))
                dve.engine_nop().then_inc(mods_ready, 1)

            def shared_weights_lo(m):
                dve.wait_ge(w_hi, m + 1)
                cols = slice(m * WCOLS, (m + 1) * WCOLS)
                split_lo(W[0][:, LO, cols], W_RAW[m], W[0][:, HI, cols]).then_inc(w_lo, 1)

            def first_weights_lo(thirds, count):
                dve.wait_ge(w_hi, count)
                for m in thirds:
                    cols = slice(m * WCOLS, (m + 1) * WCOLS)
                    split_lo(W[1][:, LO, cols], STAGE[:, cols], W[1][:, HI, cols]).then_inc(w_lo, 1)

            def ln1_apply(n, p):
                dve.wait_ge(rs1, n + 1)
                wait(dve, xt_done, n)
                for t in range(T):
                    last = dve.tensor_scalar(XN[:, t, :], X[:, p, t * D:(t + 1) * D], MV[0][:, t, 0:1],
                                             RS[0][:, t:t + 1], ALU.subtract, ALU.mult)
                last.then_inc(xn_ready, 1)

            def h1_split(n):
                dve.wait_ge(h1f_ready, n + 1)
                dve.tensor_copy(H1_T[:, HI, :, :], H1_F).then_inc(h1_hi, 1)
                dve.wait_ge(h1_hi, n + 1)
                split_lo(H1_T[:, LO, :, :], H1_F, H1_T[:, HI, :, :]).then_inc(h1_lo, 1)

            def hidden(n, fc):
                dve.wait_ge(gelu_done, n * KF + fc + 1)
                wait(dve, hid_hi, n * KF + fc - 1)
                wait(dve, hid_lo, n * KF + fc - 1)
                dve.tensor_tensor(HM[:, fc % 2, :], GEL[:, fc % 2, :], gu_bank(n, fc)[:, S:], ALU.mult).then_inc(mul_done, 1)

            def out_norm(n):
                dve.scalar_tensor_tensor(ZZ[:, :], Z[:, :], 1e-8, Z[:, :], ALU.mult, ALU.mult).then_inc(zz_ready, 1)
                dve.wait_ge(zz_ready, n + 1)
                dve.wait_ge(ssq_done, (n + 1) * T)
                dve.tensor_tensor(NSQ[:, :], ZZ[:, :], SSQ[:, :], ALU.max).then_inc(norm_sq, 1)

            def attention_out(n, p, loads):
                dve.wait_ge(mod_in[p], loads * 16)
                dve.wait_ge(fac_ready, n + 1)
                for t in range(T):
                    last = dve.scalar_tensor_tensor(TMP[:, t, :], PD[:, t * D:(t + 1) * D], FAC[:, t:t + 1],
                                                    MODB[:, p, GA, :], ALU.mult, ALU.mult)
                last.then_inc(u_read, 1)

            def ln2_stats(n, p):
                dve.wait_ge(x1_ready, n + 1)
                row_stats(lambda t: X1[:, p, t * D:(t + 1) * D], 1, st2, mv2, n)

            def ln2_centre(n, p):
                dve.wait_ge(mv2, n + 1)
                for t in range(T):
                    last = dve.scalar_tensor_tensor(TMP[:, t, :], X1[:, p, t * D:(t + 1) * D], MV[1][:, t, 0:1],
                                                    MODB[:, p, CB, :], ALU.subtract, ALU.mult)
                last.then_inc(cent2, 1)

            def ln2_apply(n, p):
                dve.wait_ge(cent2, n + 1)
                dve.wait_ge(rs2, n + 1)
                wait(dve, h2t_done, n * KD)
                wait(dve, h2_stored, n * 16)
                for t in range(T):
                    last = dve.scalar_tensor_tensor(H2[:, t, :], TMP[:, t, :], RS[1][:, t:t + 1],
                                                    MODB[:, p, SB, :], ALU.mult, ALU.add)
                last.then_inc(h2_ready, 1)

            def score_max(n, tiles):
                for t in tiles:
                    dve.wait_ge(s_done, n * T + t + 1)
                    dve.tensor_reduce(NM[:, t:t + 1], PC[:, t * S:(t + 1) * S], AX.X, ALU.max,
                                      negate=True).then_inc(nmax, 1)
                dve.wait_ge(nmax, n * T + t + 1)
                both = slice(tiles[0], tiles[1] + 1)
                dve.tensor_scalar(NB[:, both], NM[:, both], SCB[:, 5:6], SCB[:, 4:5], ALU.add,
                                  ALU.add).then_inc(ebias, 2)

            def weights_lo(n, tiles):
                for t in tiles:
                    dve.wait_ge(at_hi, n * T + t + 1)
                    split_lo(A_T[:, LO, t, :], PC[:, t * S:(t + 1) * S], A_T[:, HI, t, :]).then_inc(at_lo, 1)

            def gate_max(n):
                dve.wait_ge(gate_t_done, n + 1)
                logits = PD[:, 512:512 + T * E].rearrange("p (t e) -> p t e", t=T)
                dve.tensor_reduce(GMX[:, :], logits, AX.X, ALU.max).then_inc(gmax_ready, 1)
                dve.wait_ge(gmax_ready, n + 1)
                dve.tensor_tensor(GL[:, :, :], logits, GMX[:, :].unsqueeze(2).to_broadcast((P, T, E)),
                                  ALU.subtract).then_inc(gl_ready, 1)

            def gate_scores(n):
                dve.wait_ge(gexp_done, n + 1)
                dve.tensor_reduce(GS[:, :], GEX[:, :, :], AX.X, ALU.add).then_inc(gsum, 1)
                dve.wait_ge(gsum, n + 1)
                dve.reciprocal(GR[:, :], GS[:, :]).then_inc(grs, 1)
                dve.wait_ge(grs, n + 1)
                dve.tensor_tensor(SG[:, :, bass.ds(n, 1), :].rearrange("p t b e -> p t (b e)"), GEX[:, :, :],
                                  GR[:, :].unsqueeze(2).to_broadcast((P, T, E)), ALU.mult).then_inc(sg_ready, 1)

            def group_scores(g):
                wait_apart(dve, sg_ready, (g + 1) * GROUP)
                dve.tensor_copy(ROW[1][:, :].rearrange("p (t n) -> p t n", t=T),
                                SG[:, :, bass.ds(g * GROUP, GROUP), :].rearrange("p t b e -> p t (b e)")
                                ).then_inc(group_set, 1)

            def score_rows(g, ps):
                dve.wait_ge(sgt_ps, g + 1)
                dve.tensor_copy(ROW[0][:, :].rearrange("r (p t) -> r t p", t=T),
                                ps.rearrange("r (t p) -> r t p", t=T)).then_inc(row_ready, 1)
                wait_apart(dve, row_ready, g + 1)

            def top_best(odd):
                dve.max(BESTV[:, :], ROW[1 if odd else 0][:, :]).then_inc(top_step, 1)

            def top_strike(odd, g, r, before):
                src, dst = (ROW[1], ROW[0]) if odd else (ROW[0], ROW[1])
                wait_apart(dve, top_step, before * 3 + 1)
                dve.max_index(BESTU[:, :], BESTV[:, :], src[:, :]).then_inc(top_step, 1)
                dve.match_replace(dst[:, :], BESTV[:, :], src[:, :], -1.0).then_inc(top_step, 1)
                dve.tensor_copy(TOPV[:, :, bass.ds(r * 8, 8)], BESTV[:, :].unsqueeze(1).to_broadcast((P, 2, 8)))
                wait_apart(dve, top_step, before * 3 + 3)
                dve.tensor_scalar(TOPI[:, :, bass.ds(r * 8, 8)], BESTU[:, :].unsqueeze(1).to_broadcast((P, 2, 8)),
                                  CONST[:, bass.ds(g + C_BASE, 1)], None, ALU.add).then_inc(top_kept, 1)

            def top_slots(g, ps):
                dve.wait_ge(tops_t_ps, g + 1)
                for h in range(2):
                    rows = slice(h * CAP, (h + 1) * CAP)
                    for o, dst in ((0, IDX), (P, WGT)):
                        last = dve.tensor_copy(
                            dst[rows, :, bass.ds(g * TT, TT)],
                            ps[rows, o:o + P].rearrange("p (q h e) -> p h e q", h=2, e=E)[:, h])
                last.then_inc(tops_read, 1)

            def rows_lo(s, p):
                for k in range(KD):
                    dve.wait_ge(tx_hi, s * KD + k + 1)
                    split_lo(XT[p][:, LO, k, :], PC[:, 1024 + k * S:1024 + (k + 1) * S],
                             XT[p][:, HI, k, :]).then_inc(tx_lo, 1)

            def iteration(i, p, half, rounds=(), finish=None, start=None):
                if valid(i - 1):
                    attention_out(i - 1, 1 - p, half + p)
                if valid(i):
                    dve.wait_ge(k_hi, i + 1)
                    split_lo(K_T[:, LO, :, :].rearrange("p k s -> p (k s)"), PC[:, KD * S:],
                             K_T[:, HI, :, :].rearrange("p k s -> p (k s)")).then_inc(k_lo, 1)
                    dve.wait_ge(v_hi, i + 1)
                    split_lo(V[:, LO, :, :].rearrange("p t d -> p (t d)"), PC[:, 0:T * D],
                             V[:, HI, :, :].rearrange("p t d -> p (t d)")).then_inc(v_lo, 1)
                if at(i, 0):
                    modulations()
                    gate_weights()
                if valid(i - 2):
                    hidden(i - 2, 3)
                if at(i, B + 1):
                    first_weights_lo((0, 2), 5)
                    first_weights_lo((1,), 6)
                    rows_lo(0, 0)
                if valid(i - 1):
                    ln2_stats(i - 1, 1 - p)
                if valid(i):
                    score_max(i, (0, 1))
                if valid(i - 1):
                    ln2_centre(i - 1, 1 - p)
                if at(i, 0):
                    ln1_stats(1, 1, 1)
                if valid(i):
                    score_max(i, (2, 3))
                if at(i, 0):
                    shared_weights_lo(0)
                if valid(i - 1):
                    ln2_apply(i - 1, 1 - p)
                if valid(i - 2):
                    wait(dve, y_stored, (i - 2) * 16)
                    for bank in range(2):
                        tiles = slice(bank * 2, bank * 2 + 2)
                        dve.wait_ge(down_done, (i - 2) * 2 + bank + 1)
                        last = dve.tensor_tensor(Y[:, tiles, :],
                                                 PD[:, bank * S:(bank + 1) * S].rearrange("p (t d) -> p t d", t=2),
                                                 MODB[:, p, GB, :].unsqueeze(1).to_broadcast((P, 2, D)), ALU.mult)
                    last.then_inc(y_read, 1)
                if valid(i - 1):
                    for k in range(KD):
                        dve.wait_ge(h2t_hi, (i - 1) * KD + k + 1)
                        split_lo(H2_T[:, LO, k, :], PG[:, k * S:(k + 1) * S], H2_T[:, HI, k, :]).then_inc(h2t_lo, 1)
                if valid(i):
                    weights_lo(i, (0, 1))
                if valid(i + 1) and not at(i, -1) and not at(i, 0):
                    ln1_stats(i + 1, 1 - p, half + 1 + p)
                if valid(i):
                    weights_lo(i, (2, 3))
                if valid(i + 1):
                    ln1_apply(i + 1, 1 - p)
                if at(i, -1):
                    rotations()
                if at(i, 0):
                    shared_weights_lo(1)
                    shared_weights_lo(2)
                if valid(i - 1):
                    hidden(i - 1, 0)
                if valid(i - 2):
                    gate_scores(i - 2)
                if valid(i - 1):
                    gate_max(i - 1)
                for g, r, before in rounds[:1]:
                    odd = 0 if len(rounds) == 2 else 1 - p
                    top_best(odd)
                    top_strike(odd, g, r, before)
                if start is not None:
                    group_scores(start)
                if valid(i + 1):
                    h1_split(i + 1)
                if valid(i - 1):
                    hidden(i - 1, 1)
                if len(rounds) > 1:
                    top_best(1)
                if valid(i):
                    out_norm(i)
                for g, r, before in rounds[1:]:
                    top_strike(1, g, r, before)
                if finish is not None:
                    top_slots(finish, PC[:, 3 * S:])
                if start is not None:
                    score_rows(start, PC[:, 2 * S:3 * S])
                if valid(i - 1):
                    hidden(i - 1, 2)

            phase_a_with_tops(dve, iteration)

            dve.wait_ge(hid_hi, KF * B)
            dve.wait_ge(hid_lo, KF * B)

            def weigh(e, g, tiles):
                s = e * NG + g
                for t in tiles:
                    dve.wait_ge(edown_done, s * TT + (t // 2 + 1) * 2)
                    if t == 0:
                        wait(dve, scattered[(g - 2) % NG], (e + (1 if g >= 2 else 0)) * (TT * 16))
                    dve.scalar_tensor_tensor(X1[:, g % 2, t * D:(t + 1) * D], PD[:, t * D:(t + 1) * D],
                                             WCUR[g][:, t:t + 1], PAIRS[:, g * TT + t, :], ALU.mult,
                                             ALU.mult).then_inc(eo_ready, 1)

            def step(e, p, g, first=False, last=False):
                s = e * NG + g
                if first:
                    group_scores(NG - 1)
                    score_rows(NG - 1, PC[:, 0:S])
                if at(e, 0) and g == 1:
                    dve.wait_ge(pairs_in, 32)
                    dve.wait_ge(y_ready, B)
                if g >= 1 and not (isinstance(e, int) and e == E - 1):
                    dve.wait_ge(w_hi, e * 3 + 6 + g)
                    cols = slice((g - 1) * WCOLS, g * WCOLS)
                    split_lo(W[p][:, LO, cols], STAGE[:, cols], W[p][:, HI, cols]).then_inc(w_lo, 1)
                for fc in range(KF):
                    bank = PG if fc % 2 == 0 else PC[:, 0:1024]
                    dve.wait_ge(egelu_done, s * KF + fc + 1)
                    wait(dve, ehid_hi, s * KF + fc - 1)
                    wait(dve, ehid_lo, s * KF + fc - 1)
                    dve.tensor_tensor(HM[:, fc % 2, :], GEL[:, fc % 2, :], bank[:, S:], ALU.mult).then_inc(emul_done, 1)
                    if at(e, 0) and g < 2:
                        dve.wait_ge(top_kept, (NG - 1) * (CAP // 8) + g * KF + fc)
                        top_best(fc % 2)
                    if fc == 2 and not last:
                        rows_lo(s + 1, (g + 1) % 2)
                    dve.wait_ge(ehid_hi, s * KF + fc + 1)
                    dve.tensor_tensor(H[g % 2][:, LO, fc, :], HM[:, fc % 2, :], H[g % 2][:, HI, fc, :].bitcast(F32),
                                      ALU.subtract).then_inc(ehid_lo, 1)
                    if fc in (0, 1) and not first:
                        weigh(e if g else e - 1, (g - 1) % NG, (2 * fc, 2 * fc + 1))
                    if at(e, 0) and g == 2 and fc == 0:
                        top_slots(NG - 1, PD[:, S:])
                    if at(e, 0) and g < 2:
                        top_strike(fc % 2, NG - 1, g * KF + fc, (NG - 1) * (CAP // 8) + g * KF + fc)
                if last:
                    weigh(e, g, range(TT))

            phase_b(dve, step)

        @block.gpsimd
        def _(pool):
            pool.wait_ge(consts_in, 16)
            pool.wait_ge(rot_sq, 1)
            pool.tensor_tensor(RN[:, :, :].rearrange("p a k -> p (a k)"), RN[:, :, :].rearrange("p a k -> p (a k)"),
                               const(C_HALF, 3 * KD), ALU.pow).then_inc(rot_rn, 1)

            def rstd(j, mv, ve, rs, n):
                wait_apart(pool, mv, n + 1)
                pool.tensor_scalar(RS[j][:, :], MV[j][:, :, 1], EPS, None, ALU.add).then_inc(ve, 1)
                pool.wait_ge(ve, n + 1)
                pool.tensor_tensor(RS[j][:, :], RS[j][:, :], const(C_HALF, T), ALU.pow).then_inc(rs, 1)

            def hidden_lo(n, fc):
                pool.wait_ge(hid_hi, n * KF + fc + 1)
                pool.tensor_tensor(HID[:, LO, fc, :], HM[:, fc % 2, :], HID[:, HI, fc, :].bitcast(F32),
                                   ALU.subtract).then_inc(hid_lo, 1)

            def gather(e, g, s):
                j = g % NG
                if at(e, 0):
                    pool.wait_ge(tops_read, g + 1)
                wait(pool, tx_done, s * KD - KD)
                wait(pool, scattered[j], e * (TT * 16))
                pool.tensor_copy(ICUR[j][:, :], IDX[:, bass.ds(e, 1), g * TT:(g + 1) * TT].rearrange("p o q -> p (o q)"))
                pool.tensor_copy(WCUR[j][:, :], WGT[:, bass.ds(e, 1), g * TT:(g + 1) * TT].rearrange(
                    "p o q -> p (o q)")).then_inc(cur_ready, 1)
                wait_apart(pool, cur_ready, s + 1)
                for t in range(TT):
                    pool.indirect_dma_start(
                        out=X[:, g % 2, t * D:(t + 1) * D], out_offset=None, in_=h2_dram,
                        in_offset=bass.IndirectOffsetOnAxis(ap=ICUR[j][:, t:t + 1], axis=0)).then_inc(gathered[g % 2], 16)

            def iteration(i, p, half):
                if at(i, 1):
                    pool.wait_ge(w_lo, 3)
                if valid(i - 1):
                    pool.wait_ge(u_read, i)
                    pool.tensor_tensor(X1[:, 1 - p, :], TMP[:, :, :].rearrange("p t d -> p (t d)"), X[:, 1 - p, :],
                                       ALU.add).then_inc(x1_ready, 1)
                if valid(i - 2):
                    hidden_lo(i - 2, 3)
                if valid(i - 1):
                    rstd(1, mv2, ve2, rs2, i - 1)
                if at(i, B + 1):
                    gather(0, 1, 1)
                if valid(i + 1):
                    rstd(0, mv1, ve1, rs1, i + 1)
                if valid(i - 2):
                    pool.wait_ge(y_read, i - 1)
                    pool.tensor_tensor(Y[:, :, :].rearrange("p t d -> p (t d)"),
                                       Y[:, :, :].rearrange("p t d -> p (t d)"), X1[:, p, :],
                                       ALU.add).then_inc(y_ready, 1)
                if at(i, B):
                    pool.wait_ge(h2_stored, 16 * B)
                    pool.wait_ge(x1_ready, B)
                    gather(0, 0, 0)
                if valid(i - 1):
                    hidden_lo(i - 1, 0)
                    hidden_lo(i - 1, 1)
                if valid(i):
                    pool.wait_ge(norm_sq, i + 1)
                    pool.tensor_tensor(FAC[:, :], NSQ[:, :], const(C_HALF, T), ALU.pow).then_inc(fac_ready, 1)
                if valid(i - 1):
                    hidden_lo(i - 1, 2)

            phase_a(pool, iteration)

            def scatter(e, g, s, last=False):
                for t in range(TT):
                    if t == 0 and not last:
                        wait_apart(pool, eo_ready, (s + 1) * TT)
                    if last:
                        pool.wait_ge(eo_ready, s * TT + t + 1)
                    pool.indirect_dma_start(
                        out=out_rows, out_offset=bass.IndirectOffsetOnAxis(ap=ICUR[g][:, t:t + 1], axis=0),
                        in_=X1[:, g % 2, t * D:(t + 1) * D], in_offset=None,
                        compute_op=ALU.add).then_inc(scattered[g], 16)

            def step(e, p, g, first=False, last=False):
                s = e * NG + g
                if at(e, 0) and g == 1:
                    pool.wait_ge(y_stored, 16 * B)
                if not last and not first:
                    en, gn = (e, g + 1) if g + 1 < NG else (e + 1, 0)
                    gather(en, gn, s + 1)
                if not first:
                    ep, gp = (e, g - 1) if g else (e - 1, NG - 1)
                    scatter(ep, gp, s - 1)
                if last:
                    scatter(e, g, s, last=True)

            phase_b(pool, step)
            for g in range(NG):
                pool.wait_ge(scattered[g], E * TT * 16)


def kernel(**inputs):
    import numpy as np
    import concourse.bacc as bacc
    from concourse.bass_utils import run_bass_kernel_spmd

    a = {k: np.asarray(v) for k, v in inputs.items()}

    def in_features(w):
        w = np.swapaxes(w, -1, -2)
        lead, (i, o) = w.shape[:-2], w.shape[-2:]
        w = w.reshape(*lead, i // P, P, o)
        return np.ascontiguousarray(np.swapaxes(w, -2, -3).reshape(*lead, P, i // P * o))

    consts = np.zeros((P, C_ALL), np.float32)
    rows = np.arange(P)
    consts[:, C_ID:C_ID + P] = np.eye(P)
    consts[rows, C_SWAP + (rows ^ 1)] = 1
    consts[:, C_EVEN] = rows % 2 == 0
    consts[:, C_ODD] = rows % 2 == 1
    consts[:, C_SIGN] = 1 - 2 * (rows % 2)
    consts[:, C_BASE:C_BASE + NG] = (rows[:, None] // E + GROUP * np.arange(NG)) * S
    consts[:, C_HALF:] = -0.5

    arrays = {
        "x": a["L0_attn_Q"],
        "rot": np.ascontiguousarray(a["L0_attn_rot_w"].reshape(3, KD, P).transpose(2, 0, 1).reshape(P, 3 * KD)),
        "scale": a["L0_attn_scale"].reshape(1, 1),
        "bias": a["L0_attn_bias"].reshape(1, 1),
        "gate_t": in_features(a["L0_ffn_gate_w"]),
        "wg": in_features(a["L0_ffn_Wg"]),
        "wu": in_features(a["L0_ffn_Wu"]),
        "wd": in_features(a["L0_ffn_Wd"]),
        "wsg": in_features(a["L0_ffn_Ws_g"]),
        "wsu": in_features(a["L0_ffn_Ws_u"]),
        "wsd": in_features(a["L0_ffn_Ws_d"]),
        "c": a["L0_c"],
        "wmod": a["L0_wmod"],
        "consts": consts,
    }
    nc = bacc.Bacc("TRN2", target_bir_lowering=False, num_devices=1)
    arrays = {k: np.ascontiguousarray(v) for k, v in arrays.items()}
    dram = {k: nc.dram_tensor(f"in_{k}", v.shape, mybir.dt.from_np(v.dtype), kind="ExternalInput").ap()
            for k, v in arrays.items()}
    out = nc.dram_tensor("out_0", (B, S, D), F32, kind="ExternalOutput").ap()
    block_kernel(nc, dram["x"], dram["rot"], dram["scale"], dram["bias"], dram["gate_t"],
                 (dram["wg"], dram["wu"], dram["wd"]), (dram["wsg"], dram["wsu"], dram["wsd"]),
                 dram["c"], dram["wmod"], dram["consts"], out)
    r = run_bass_kernel_spmd(nc, [{f"in_{k}": v for k, v in arrays.items()}], core_ids=[0])
    return r.results[0]["out_0"]
```
